# Optimizing a Trainium2 kernel written in Bass

```python
import numpy as np
import jax
import jax.numpy as jnp

def _softmax(x, axis=-1):
    return jax.nn.softmax(x, axis=axis)

def _gelu(x):
    return jax.nn.gelu(x, approximate=True)

def _silu(x):
    return jax.nn.silu(x)

def _sigmoid(x):
    return jax.nn.sigmoid(x)

def _layernorm(x, axis=-1, eps=1e-05):
    m = jnp.mean(x, axis=axis, keepdims=True)
    v = jnp.var(x, axis=axis, keepdims=True)
    return (x - m) / jnp.sqrt(v + eps)

def _scatter_add(tgt, idx, src, axis=0):
    return tgt.at[idx].add(src)

def _segment_sum(src, seg, n):
    return jax.ops.segment_sum(src, seg, n)
kernel_name = 'mk_xattn_seq_d2_seqx_r8_d480f5'

def setup_inputs(seed: int=0):
    np.random.seed(seed)
    _w = jnp.asarray

    def _rec_inputs():
        import jax
        import jax.numpy as jnp
        _rk = jax.random.key(seed)
        x = -0.0002928 + 1 * jax.random.normal(jax.random.fold_in(_rk, 1), (8, 256, 128), jnp.float32)
        _lenS = 256 - jax.random.randint(jax.random.fold_in(_rk, 7), (8,), 0, max(1, 256 // 4) + 1, jnp.int32)
        _lenS2 = 256 - jax.random.randint(jax.random.fold_in(_rk, 8), (8,), 0, max(1, 256 // 4) + 1, jnp.int32)
        _ctx_1024P = jax.random.normal(jax.random.fold_in(_rk, 11), (8, 16, 128), jnp.float32)
        _ctx_1024c = jax.random.dirichlet(jax.random.fold_in(_rk, 511), 0.3 * jnp.ones((16,), jnp.float32), (8, 256))
        _ctx_1024t = jnp.einsum('bsk,bkd->bsd', _ctx_1024c, _ctx_1024P)
        _ctx_1024t = _ctx_1024t * jax.lax.rsqrt(jnp.mean(jnp.square(_ctx_1024t)) + 1e-12) * 0.953939
        ctx_1024 = -1.39393e-06 + 0.999914 * (_ctx_1024t + 0.3 * jax.random.normal(jax.random.fold_in(_rk, 611), (8, 256, 128), jnp.float32))
        fside_1x16xSxS2_0 = 8.74812e-06 + 0.100005 * jax.random.normal(jax.random.fold_in(_rk, 13), (1, 16, 256, 256), jnp.float32)
        _validS = jnp.arange(256)[None, :] < _lenS[:, None]
        _validS2 = jnp.arange(256)[None, :] < _lenS2[:, None]
        _causal = jnp.tril(jnp.ones((256, 256), dtype=bool))
        mask_BxSxS2_bk1 = jnp.broadcast_to(_validS2[:, None, :], (8, 256, 256))
        mask_BxSxS2_bk0 = jnp.logical_not(jnp.broadcast_to(_validS2[:, None, :], (8, 256, 256)))
        return (x, ctx_1024, fside_1x16xSxS2_0, mask_BxSxS2_bk1, mask_BxSxS2_bk0)
    x, ctx_1024, fside_1x16xSxS2_0, mask_BxSxS2_bk1, mask_BxSxS2_bk0 = _rec_inputs()

    def _L0_xattn_setup():
        import jax, jax.numpy as jnp
        import numpy as np
        B, L, S, D, H, FF = (2, 256, 256, 128, 16, 512)
        HD = D // H
        TEMP = float(D) ** 0.5
        EPS = 1e-05

        def _layernorm(x, g, b):
            mu = jnp.mean(x, axis=-1, keepdims=True)
            var = jnp.mean(jnp.square(x - mu), axis=-1, keepdims=True)
            return (x - mu) * jax.lax.rsqrt(var + EPS) * g + b

        def _mha(q_in, k_in, v_in, wq, bq, wk, bk, wv, bv, wo, bo, mask, bias):
            b, ql = (q_in.shape[0], q_in.shape[1])
            kl = k_in.shape[1]
            q = (q_in @ wq + bq).reshape(b, ql, H, HD).transpose(0, 2, 1, 3)
            k = (k_in @ wk + bk).reshape(b, kl, H, HD).transpose(0, 2, 1, 3)
            v = (v_in @ wv + bv).reshape(b, kl, H, HD).transpose(0, 2, 1, 3)
            attn = jnp.einsum('bhqd,bhkd->bhqk', q, k) / TEMP
            if bias is not None:
                attn = attn + bias
            if mask is not None:
                attn = jnp.where(mask[:, None, :, :], -jnp.inf, attn)
            attn = jax.nn.softmax(attn, axis=-1)
            out = jnp.einsum('bhqk,bhkd->bhqd', attn, v)
            out = out.transpose(0, 2, 1, 3).reshape(b, ql, H * HD)
            return out @ wo + bo
        key = jax.random.key(seed)
        ks = jax.random.split(key, 32)
        w = lambda k, shape, s=0.02: jax.random.normal(k, shape, jnp.float32) * s
        inp = {}
        inp['tgt'] = jax.random.normal(ks[0], (B, L, D), jnp.float32)
        inp['src'] = jax.random.normal(ks[1], (B, S, D), jnp.float32)
        causal = jnp.triu(jnp.ones((L, L), dtype=bool), 1)
        inp['tgt_mask'] = jnp.broadcast_to(causal, (B, L, L))
        inp['attn_bias'] = w(ks[2], (1, H, L, L), 0.1)
        inp['attn_2d_bias'] = w(ks[3], (1, H, L, S), 0.1)
        inp['sa_wq'] = w(ks[4], (D, D))
        inp['sa_bq'] = jnp.zeros((D,))
        inp['sa_wk'] = w(ks[5], (D, D))
        inp['sa_bk'] = jnp.zeros((D,))
        inp['sa_wv'] = w(ks[6], (D, D))
        inp['sa_bv'] = jnp.zeros((D,))
        inp['sa_wo'] = w(ks[7], (D, D))
        inp['sa_bo'] = jnp.zeros((D,))
        inp['sa_g'] = jnp.ones((D,))
        inp['sa_b'] = jnp.zeros((D,))
        inp['ca_wq'] = w(ks[8], (D, D))
        inp['ca_bq'] = jnp.zeros((D,))
        inp['ca_wk'] = w(ks[9], (D, D))
        inp['ca_bk'] = jnp.zeros((D,))
        inp['ca_wv'] = w(ks[10], (D, D))
        inp['ca_bv'] = jnp.zeros((D,))
        inp['ca_wo'] = w(ks[11], (D, D))
        inp['ca_bo'] = jnp.zeros((D,))
        inp['ca_g'] = jnp.ones((D,))
        inp['ca_b'] = jnp.zeros((D,))
        inp['ff_w1'] = w(ks[12], (D, FF))
        inp['ff_b1'] = jnp.zeros((FF,))
        inp['ff_w2'] = w(ks[13], (FF, D))
        inp['ff_b2'] = jnp.zeros((D,))
        inp['ff_g'] = jnp.ones((D,))
        inp['ff_b'] = jnp.zeros((D,))
        return inp
    _L0_xattn_all = _L0_xattn_setup()
    _L0_xattn_in = {k: v for k, v in _L0_xattn_all.items() if k in ('attn_2d_bias', 'sa_wq', 'sa_bq', 'sa_wk', 'sa_bk', 'sa_wv', 'sa_bv', 'sa_wo', 'sa_bo', 'sa_g', 'sa_b', 'ca_wq', 'ca_bq', 'ca_wk', 'ca_bk', 'ca_wv', 'ca_bv', 'ca_wo', 'ca_bo', 'ca_g', 'ca_b', 'ff_w1', 'ff_b1', 'ff_w2', 'ff_b2', 'ff_g', 'ff_b')}
    del _L0_xattn_all

    def _L1_xattn_setup():
        import jax, jax.numpy as jnp
        import numpy as np
        EPS = 1e-05

        def layer_norm(x, w, b):
            mu = jnp.mean(x, axis=-1, keepdims=True)
            var = jnp.var(x, axis=-1, keepdims=True)
            return (x - mu) * jax.lax.rsqrt(var + EPS) * w + b
        key = jax.random.key(seed)
        ks = jax.random.split(key, 12)
        B, N, M, C = (2, 256, 256, 128)
        H = 16
        hid = 4 * C
        s = lambda d: 1.0 / np.sqrt(d)
        return {'x': jax.random.normal(ks[0], (B, N, C), jnp.float32), 'context': jax.random.normal(ks[1], (B, M, C), jnp.float32), 'xa_mask': jax.random.bernoulli(ks[2], 0.1, (B, N, M)), 'qn_w': jnp.ones((C,), jnp.float32), 'qn_b': jnp.zeros((C,), jnp.float32), 'cn_w': jnp.ones((C,), jnp.float32), 'cn_b': jnp.zeros((C,), jnp.float32), 'n2_w': jnp.ones((C,), jnp.float32), 'n2_b': jnp.zeros((C,), jnp.float32), 'q_w': jax.random.normal(ks[3], (C, C), jnp.float32) * s(C), 'kv_w': jax.random.normal(ks[4], (C, 2 * C), jnp.float32) * s(C), 'proj_w': jax.random.normal(ks[5], (C, C), jnp.float32) * s(C), 'proj_b': jnp.zeros((C,), jnp.float32), 'fc1_w': jax.random.normal(ks[6], (C, hid), jnp.float32) * s(C), 'fc1_b': jnp.zeros((hid,), jnp.float32), 'fc2_w': jax.random.normal(ks[7], (hid, C), jnp.float32) * s(hid), 'fc2_b': jnp.zeros((C,), jnp.float32)}
    _L1_xattn_all = _L1_xattn_setup()
    _L1_xattn_in = {k: v for k, v in _L1_xattn_all.items() if k in ('qn_w', 'qn_b', 'cn_w', 'cn_b', 'n2_w', 'n2_b', 'q_w', 'kv_w', 'proj_w', 'proj_b', 'fc1_w', 'fc1_b', 'fc2_w', 'fc2_b')}
    del _L1_xattn_all
    return {'x': x, 'ctx_1024': ctx_1024, 'fside_1x16xSxS2_0': fside_1x16xSxS2_0, 'mask_BxSxS2_bk1': mask_BxSxS2_bk1, 'mask_BxSxS2_bk0': mask_BxSxS2_bk0, 'L0_xattn_attn_2d_bias': _L0_xattn_in['attn_2d_bias'], 'L0_xattn_sa_wq': _L0_xattn_in['sa_wq'], 'L0_xattn_sa_bq': _L0_xattn_in['sa_bq'], 'L0_xattn_sa_wk': _L0_xattn_in['sa_wk'], 'L0_xattn_sa_bk': _L0_xattn_in['sa_bk'], 'L0_xattn_sa_wv': _L0_xattn_in['sa_wv'], 'L0_xattn_sa_bv': _L0_xattn_in['sa_bv'], 'L0_xattn_sa_wo': _L0_xattn_in['sa_wo'], 'L0_xattn_sa_bo': _L0_xattn_in['sa_bo'], 'L0_xattn_sa_g': _L0_xattn_in['sa_g'], 'L0_xattn_sa_b': _L0_xattn_in['sa_b'], 'L0_xattn_ca_wq': _L0_xattn_in['ca_wq'], 'L0_xattn_ca_bq': _L0_xattn_in['ca_bq'], 'L0_xattn_ca_wk': _L0_xattn_in['ca_wk'], 'L0_xattn_ca_bk': _L0_xattn_in['ca_bk'], 'L0_xattn_ca_wv': _L0_xattn_in['ca_wv'], 'L0_xattn_ca_bv': _L0_xattn_in['ca_bv'], 'L0_xattn_ca_wo': _L0_xattn_in['ca_wo'], 'L0_xattn_ca_bo': _L0_xattn_in['ca_bo'], 'L0_xattn_ca_g': _L0_xattn_in['ca_g'], 'L0_xattn_ca_b': _L0_xattn_in['ca_b'], 'L0_xattn_ff_w1': _L0_xattn_in['ff_w1'], 'L0_xattn_ff_b1': _L0_xattn_in['ff_b1'], 'L0_xattn_ff_w2': _L0_xattn_in['ff_w2'], 'L0_xattn_ff_b2': _L0_xattn_in['ff_b2'], 'L0_xattn_ff_g': _L0_xattn_in['ff_g'], 'L0_xattn_ff_b': _L0_xattn_in['ff_b'], 'L1_xattn_qn_w': _L1_xattn_in['qn_w'], 'L1_xattn_qn_b': _L1_xattn_in['qn_b'], 'L1_xattn_cn_w': _L1_xattn_in['cn_w'], 'L1_xattn_cn_b': _L1_xattn_in['cn_b'], 'L1_xattn_n2_w': _L1_xattn_in['n2_w'], 'L1_xattn_n2_b': _L1_xattn_in['n2_b'], 'L1_xattn_q_w': _L1_xattn_in['q_w'], 'L1_xattn_kv_w': _L1_xattn_in['kv_w'], 'L1_xattn_proj_w': _L1_xattn_in['proj_w'], 'L1_xattn_proj_b': _L1_xattn_in['proj_b'], 'L1_xattn_fc1_w': _L1_xattn_in['fc1_w'], 'L1_xattn_fc1_b': _L1_xattn_in['fc1_b'], 'L1_xattn_fc2_w': _L1_xattn_in['fc2_w'], 'L1_xattn_fc2_b': _L1_xattn_in['fc2_b']}

def reference(x, ctx_1024, fside_1x16xSxS2_0, mask_BxSxS2_bk1, mask_BxSxS2_bk0, L0_xattn_attn_2d_bias, L0_xattn_sa_wq, L0_xattn_sa_bq, L0_xattn_sa_wk, L0_xattn_sa_bk, L0_xattn_sa_wv, L0_xattn_sa_bv, L0_xattn_sa_wo, L0_xattn_sa_bo, L0_xattn_sa_g, L0_xattn_sa_b, L0_xattn_ca_wq, L0_xattn_ca_bq, L0_xattn_ca_wk, L0_xattn_ca_bk, L0_xattn_ca_wv, L0_xattn_ca_bv, L0_xattn_ca_wo, L0_xattn_ca_bo, L0_xattn_ca_g, L0_xattn_ca_b, L0_xattn_ff_w1, L0_xattn_ff_b1, L0_xattn_ff_w2, L0_xattn_ff_b2, L0_xattn_ff_g, L0_xattn_ff_b, L1_xattn_qn_w, L1_xattn_qn_b, L1_xattn_cn_w, L1_xattn_cn_b, L1_xattn_n2_w, L1_xattn_n2_b, L1_xattn_q_w, L1_xattn_kv_w, L1_xattn_proj_w, L1_xattn_proj_b, L1_xattn_fc1_w, L1_xattn_fc1_b, L1_xattn_fc2_w, L1_xattn_fc2_b):
    import jax
    import jax.numpy as jnp

    def _L0_xattn_ref(tgt, src, tgt_mask, attn_bias, attn_2d_bias, sa_wq, sa_bq, sa_wk, sa_bk, sa_wv, sa_bv, sa_wo, sa_bo, sa_g, sa_b, ca_wq, ca_bq, ca_wk, ca_bk, ca_wv, ca_bv, ca_wo, ca_bo, ca_g, ca_b, ff_w1, ff_b1, ff_w2, ff_b2, ff_g, ff_b):
        import jax, jax.numpy as jnp
        import numpy as np
        B, L, S, D, H, FF = (2, 256, 256, 128, 16, 512)
        HD = D // H
        TEMP = float(D) ** 0.5
        EPS = 1e-05

        def _layernorm(x, g, b):
            mu = jnp.mean(x, axis=-1, keepdims=True)
            var = jnp.mean(jnp.square(x - mu), axis=-1, keepdims=True)
            return (x - mu) * jax.lax.rsqrt(var + EPS) * g + b

        def _mha(q_in, k_in, v_in, wq, bq, wk, bk, wv, bv, wo, bo, mask, bias):
            b, ql = (q_in.shape[0], q_in.shape[1])
            kl = k_in.shape[1]
            q = (q_in @ wq + bq).reshape(b, ql, H, HD).transpose(0, 2, 1, 3)
            k = (k_in @ wk + bk).reshape(b, kl, H, HD).transpose(0, 2, 1, 3)
            v = (v_in @ wv + bv).reshape(b, kl, H, HD).transpose(0, 2, 1, 3)
            attn = jnp.einsum('bhqd,bhkd->bhqk', q, k) / TEMP
            if bias is not None:
                attn = attn + bias
            if mask is not None:
                attn = jnp.where(mask[:, None, :, :], -jnp.inf, attn)
            attn = jax.nn.softmax(attn, axis=-1)
            out = jnp.einsum('bhqk,bhkd->bhqd', attn, v)
            out = out.transpose(0, 2, 1, 3).reshape(b, ql, H * HD)
            return out @ wo + bo
        att = _mha(tgt, tgt, tgt, sa_wq, sa_bq, sa_wk, sa_bk, sa_wv, sa_bv, sa_wo, sa_bo, tgt_mask, attn_bias)
        out = _layernorm(att + tgt, sa_g, sa_b)
        att = _mha(tgt, src, src, ca_wq, ca_bq, ca_wk, ca_bk, ca_wv, ca_bv, ca_wo, ca_bo, None, attn_2d_bias)
        out = _layernorm(att + out, ca_g, ca_b)
        ff = jax.nn.relu(jax.nn.relu(out @ ff_w1 + ff_b1) @ ff_w2 + ff_b2)
        out = _layernorm(ff + out, ff_g, ff_b)
        return out

    def _L1_xattn_ref(x, context, xa_mask, qn_w, qn_b, cn_w, cn_b, n2_w, n2_b, q_w, kv_w, proj_w, proj_b, fc1_w, fc1_b, fc2_w, fc2_b):
        import jax, jax.numpy as jnp
        import numpy as np
        EPS = 1e-05

        def layer_norm(x, w, b):
            mu = jnp.mean(x, axis=-1, keepdims=True)
            var = jnp.var(x, axis=-1, keepdims=True)
            return (x - mu) * jax.lax.rsqrt(var + EPS) * w + b
        B, N, C = x.shape
        M = context.shape[1]
        H = 16
        D = C // H
        scale = D ** (-0.5)
        xq = layer_norm(x, qn_w, qn_b)
        ctx = layer_norm(context, cn_w, cn_b)
        q = (xq @ q_w).reshape(B, N, H, D)
        kv = (ctx @ kv_w).reshape(B, M, 2, H, D)
        k, v = (kv[:, :, 0], kv[:, :, 1])
        attn = jnp.einsum('bnhd,bmhd->bhnm', q, k) * scale
        neg = -jnp.finfo(attn.dtype).max
        attn = jnp.where(xa_mask[:, None, :, :], neg, attn)
        attn = jax.nn.softmax(attn, axis=-1)
        out = jnp.einsum('bhnm,bmhd->bnhd', attn, v).reshape(B, N, C)
        out = out @ proj_w + proj_b
        x = x + out
        h = layer_norm(x, n2_w, n2_b)
        h = jax.nn.gelu(h @ fc1_w + fc1_b, approximate=False) @ fc2_w + fc2_b
        return x + h
    x = _L0_xattn_ref(x, ctx_1024, mask_BxSxS2_bk1, fside_1x16xSxS2_0, L0_xattn_attn_2d_bias, L0_xattn_sa_wq, L0_xattn_sa_bq, L0_xattn_sa_wk, L0_xattn_sa_bk, L0_xattn_sa_wv, L0_xattn_sa_bv, L0_xattn_sa_wo, L0_xattn_sa_bo, L0_xattn_sa_g, L0_xattn_sa_b, L0_xattn_ca_wq, L0_xattn_ca_bq, L0_xattn_ca_wk, L0_xattn_ca_bk, L0_xattn_ca_wv, L0_xattn_ca_bv, L0_xattn_ca_wo, L0_xattn_ca_bo, L0_xattn_ca_g, L0_xattn_ca_b, L0_xattn_ff_w1, L0_xattn_ff_b1, L0_xattn_ff_w2, L0_xattn_ff_b2, L0_xattn_ff_g, L0_xattn_ff_b)
    x = _L1_xattn_ref(x, ctx_1024, mask_BxSxS2_bk0, L1_xattn_qn_w, L1_xattn_qn_b, L1_xattn_cn_w, L1_xattn_cn_b, L1_xattn_n2_w, L1_xattn_n2_b, L1_xattn_q_w, L1_xattn_kv_w, L1_xattn_proj_w, L1_xattn_proj_b, L1_xattn_fc1_w, L1_xattn_fc1_b, L1_xattn_fc2_w, L1_xattn_fc2_b)
    return x

_drawn_inputs = setup_inputs


def setup_inputs(seed=0):
    import zlib

    import numpy as np

    out = dict(_drawn_inputs(seed))
    spreads = {'L0_xattn_sa_bq': (0.0, 2.0),
     'L0_xattn_sa_bk': (0.0, 2.0),
     'L0_xattn_sa_bv': (0.0, 0.401),
     'L0_xattn_sa_bo': (0.0, 0.1),
     'L0_xattn_sa_g': (1.0, 0.2),
     'L0_xattn_sa_b': (0.0, 0.1),
     'L0_xattn_ca_bq': (0.0, 2.0),
     'L0_xattn_ca_bk': (0.0, 2.0),
     'L0_xattn_ca_bv': (0.0, 0.46),
     'L0_xattn_ca_bo': (0.0, 0.1),
     'L0_xattn_ca_g': (1.0, 0.2),
     'L0_xattn_ca_b': (0.0, 0.1),
     'L0_xattn_ff_b1': (0.0, 0.463),
     'L0_xattn_ff_b2': (0.0, 0.1),
     'L0_xattn_ff_g': (1.0, 0.2),
     'L0_xattn_ff_b': (0.0, 0.1),
     'L1_xattn_qn_w': (1.0, 0.2),
     'L1_xattn_qn_b': (0.0, 0.415),
     'L1_xattn_cn_w': (1.0, 0.2),
     'L1_xattn_cn_b': (0.0, 0.1),
     'L1_xattn_n2_w': (1.0, 0.2),
     'L1_xattn_n2_b': (0.0, 0.1),
     'L1_xattn_proj_b': (0.0, 0.1),
     'L1_xattn_fc1_b': (0.0, 0.1),
     'L1_xattn_fc2_b': (0.0, 0.1)}
    factors = {'fside_1x16xSxS2_0': 8.0,
     'L0_xattn_attn_2d_bias': 56.344,
     'L0_xattn_sa_wq': 8.0,
     'L0_xattn_sa_wk': 8.0,
     'L0_xattn_sa_wv': 5.61,
     'L0_xattn_ca_wq': 23.435,
     'L0_xattn_ca_wk': 8.0,
     'L0_xattn_ca_wv': 2.783}
    for name, (base, spread) in spreads.items():
        noise = np.random.default_rng([zlib.crc32(name.encode()), seed]).standard_normal(out[name].shape)
        drawn = base * np.exp(spread * noise) if base else spread * noise
        out[name] = jnp.asarray(drawn.astype(out[name].dtype))
    for name, factor in factors.items():
        out[name] = (out[name] * factor).astype(out[name].dtype)
    return out
```

```python
import concourse.bass as bass
from concourse import mybir
from contextlib import ExitStack


B, S, D, H, F = 8, 256, 128, 16, 512
P = 128
HD = D // H
NT = S // P
HG = 4
NG = H // HG
PARTS = 4
EPS = 1e-5
MASKED = -2.0 ** 100
SCALE = {"A": float(D) ** -0.5, "C": float(D) ** -0.5, "L": float(HD) ** -0.5}

WEIGHTS = ["Aq", "Ak", "Av", "Cq", "Ck", "Cv", "Ao", "Co", "Lq", "Lk", "Lv", "Lo"]
W_FF = {"w1": 12 * D, "w2": 12 * D + F, "fc1": 12 * D + 2 * F, "fc2": 12 * D + 3 * F}
W_COLS = 12 * D + 4 * F
COLUMN = {"Aq": 0, "Ak": 1, "Cq": 2, "Ck": 3, "b1": 4, "fc1_b": 8}
N_COLUMN = 12
VECTORS = ["Av_b", "Cv_b", "Ao_b", "Co_b", "Lo_b", "ln_A_g", "ln_A_b", "ln_C_g", "ln_C_b", "ln_F_g", "ln_F_b",
           "ln_Q_g", "ln_Q_b", "ln_K_g", "ln_K_b", "ln_N_g", "ln_N_b", "ff_b2", "fc2_b"]

LEAD_S, LEAD_M, LEAD_E = 3, 2, 1
S_BANKS, T_BANKS = 3, 2
COPY_ON_DVE = (1, 3)

STEPS = {
    "first": {2: [("v", "C", 1, 0), ("qk", "C", 1, 0)], 4: [("sel", "C", 1, 0), ("sel", "C", 1, 1)],
              6: [("sel", "C", 1, 2), ("sel", "C", 1, 3)], 7: [("fin", "A", 1, 0)], 11: [("fin", "A", 1, 1)],
              12: [("ready", "C", 1, 0)], 15: [("fin", "A", 1, 2)]},
    "C": {3: [("fin", "A", 0, 3)], 4: [("oT", "A", 0, 0)], 5: [("oproj", "A", 0, 0)],
          6: [("v", "A", 1, 0), ("qk", "A", 1, 0)], 7: [("fin", "C", 0, 0)], 8: [("sel", "A", 1, 0), ("sel", "A", 1, 1)],
          9: [("sel", "A", 1, 2), ("sel", "A", 1, 3)], 11: [("fin", "C", 0, 1)],
          12: [("maskA", "A", 1, 0), ("ready", "A", 1, 0)], 15: [("fin", "C", 0, 2)]},
    "L": {3: [("fin", "C", 0, 3)], 4: [("oT", "C", 0, 0), ("resA", "A", 1, 0)], 5: [("oproj", "C", 0, 0)],
          6: [("v", "C", 1, 0), ("qk", "C", 1, 0)], 7: [("fin", "L", -1, 0)], 8: [("sel", "C", 1, 0), ("sel", "C", 1, 1)],
          9: [("ffT", "F", 0, 0)], 10: [("ff1", "F", 0, 0), ("ff1", "F", 0, 1)], 11: [("fin", "L", -1, 1)],
          12: [("sel", "C", 1, 2), ("sel", "C", 1, 3)], 13: [("ff2", "F", 0, 0)],
          15: [("fin", "L", -1, 2), ("ready", "C", 1, 0)]},
    "A": {1: [("lnK", "K", 0, 0)], 3: [("fin", "L", -1, 3)], 4: [("oT", "L", -1, 0), ("lnQ", "Q", 0, 0)],
          5: [("oproj", "L", -1, 0)], 6: [("resL", "L", 0, 0)], 7: [("fin", "A", 1, 0)], 8: [("lT", "L", 0, 0)],
          9: [("v", "L", 0, 0), ("qk", "L", 0, 0)], 11: [("fin", "A", 1, 1), ("sel", "L", 0, 0), ("sel", "L", 0, 1)],
          12: [("sel", "L", 0, 2), ("sel", "L", 0, 3), ("maskL", "L", 0, 0)],
          15: [("fin", "A", 1, 2), ("ready", "L", 0, 0)]},
}
NO_PSUM = ("maskA", "maskL", "resA", "resL", "lnK", "lnQ", "ready")
PREPARE = [("v", 0), ("qk", 0), ("sel", 0), ("sel", 1), ("sel", 2), ("sel", 3)]


def stages(kind, i, h):
    known = isinstance(i, int)
    return [(s, j, i + d, p) for s, j, d, p in STEPS[kind].get(h, []) if not known or 0 <= i + d < B]


def number_stage_banks():
    found, before = {}, [0, 0]

    def segment(uses):
        for n, use in enumerate(uses):
            found[use] = (n % 2, before[n % 2])
            before[n % 2] += 1

    def of(kind, i):
        return [u for h in range(H) for u in stages(kind, i, h) if u[0] not in NO_PSUM]

    segment([(s, "A", 0, p) for s, p in PREPARE] + of("first", -1) + of("C", 0) + of("L", 0) + of("A", 0))
    for i in range(1, B - 1):
        segment(of("C", i) + of("L", i) + of("A", i))
    segment(of("C", B - 1) + of("L", B - 1) + of("A", B - 1) + of("L", B) + of("A", B))
    return found


USES = number_stage_banks()


def two_layers(nc: bass.Bass, t_x, t_xT, t_c, t_cT, t_mask_a, t_mask_l, t_bias_a, t_bias_c, t_weights, t_columns,
               t_vectors, t_select, t_identity, t_out):
    f32, f32r, bf16, u8 = mybir.dt.float32, mybir.dt.float32r, mybir.dt.bfloat16, mybir.dt.uint8
    ALU, ACT = mybir.AluOpType, mybir.ActivationFunctionType

    with ExitStack() as ctx:
        def sb(name, shape, dt=f32):
            return ctx.enter_context(nc.sbuf_tensor(name, shape, dt))

        def bank(name):
            return ctx.enter_context(nc.psum_tensor(name, [P, 512], f32))

        def sem(name):
            return ctx.enter_context(nc.semaphore(name))

        bias = {"A": sb("bias_a", [P, H, NT, S]), "C": sb("bias_c", [P, H, NT, S])}
        q_stack = {j: sb(f"q_stack_{j}", [P, NG, S], f32r) for j in "ACL"}
        k_stack = {j: sb(f"k_stack_{j}", [P, NG, S], f32r) for j in "ACL"}
        values = {j: sb(f"values_{j}", [P, NT, H, 32]) for j in "ACL"}
        neg_scores = sb("neg_scores", [P, 4, NT, S])
        neg_max_a = sb("neg_max_a", [P, NT, H])
        neg_max_cl = sb("neg_max_cl", [P, NT, H])
        probs = sb("probs", [P, 2, NT, S])
        probsT = sb("probsT", [P, 2, HG, NT, S])
        headsT = sb("headsT", [P, 2, S])
        sums = sb("sums", [P, NT, HG])
        inverse = sb("inverse", [P, NT, HG])
        attended = {j: sb(f"attended_{j}", [P, NT, D]) for j in "ACL"}
        attendedT = sb("attendedT", [P, S])
        qk_plain = sb("qk_plain", [P, 2, S])
        qk_high = sb("qk_high", [P, 2, S], f32r)
        qk_low = sb("qk_low", [P, 2, S], f32r)
        weights = sb("weights", [P, W_COLS])
        columns = sb("columns", [P, N_COLUMN])
        vectors = sb("vectors", [P, len(VECTORS), D])
        select = sb("select", [P, PARTS, NG, P], f32r)
        identity = sb("identity", [P, P])
        identity16 = sb("identity16", [P, P], bf16)
        xT, cT = sb("xT", [P, S]), sb("cT", [P, S])
        x_tok, c_tok = sb("x_tok", [P, NT, D]), sb("c_tok", [P, NT, D])
        mask_a8, mask_l8 = sb("mask_a8", [P, NT, S], u8), sb("mask_l8", [P, NT, S], u8)
        mask_a, mask_l = sb("mask_a", [P, NT, S], bf16), sb("mask_l", [P, NT, S], bf16)
        residual = {j: sb(f"residual_{j}", [P, NT, D]) for j in "ACL"}
        summed = sb("summed", [P, NT, D])
        ff_out = sb("ff_out", [P, NT, D])
        normed = {k: sb(f"normed_{k}", [P, NT, D]) for k in "ACFQK"}
        stats = {k: sb(f"stats_{k}", [P, NT, 6]) for k in "ACFQKN"}
        minus_half = sb("minus_half", [P, NT])
        mean_var = {k: sb(f"mean_var_{k}", [P, NT, 2]) for k in "ACFQKN"}
        rstd = {k: sb(f"rstd_{k}", [P, NT]) for k in "ACFQKN"}
        ffT = sb("ffT", [P, S])
        hiddenT = sb("hiddenT", [P, F // P, S])
        lT = sb("lT", [P, 2, S])
        x2 = sb("x2", [P, B, NT, D])

        def vec(name):
            return vectors[:, VECTORS.index(name), :]

        def vec2(name):
            return vectors[:, VECTORS.index(name):VECTORS.index(name) + 1, :].broadcast_to([P, NT, D])

        def weight(name):
            n = WEIGHTS.index(name)
            return weights[:, n * D:(n + 1) * D]

        score_bank = [bank(f"score_bank{n}") for n in range(S_BANKS)]
        turn_bank = [bank(f"turn_bank{n}") for n in range(T_BANKS)]
        head_bank = bank("head_bank")
        stage_bank = [bank(f"stage_bank{n}") for n in range(2)]

        scores_ready = sem("scores_ready")
        maxima_ready = sem("maxima_ready")
        exps_ready = sem("exps_ready")
        turned = sem("turned")
        copied_act = sem("copied_act")
        copied_dve = sem("copied_dve")
        heads_ready = sem("heads_ready")
        heads_copied = sem("heads_copied")
        fin_steps = sem("fin_steps")
        stage_filled = [sem(f"stage_filled{n}") for n in range(2)]
        stage_read = [sem(f"stage_read{n}") for n in range(2)]
        split_done = {j: sem(f"split_done_{j}") for j in "ACL"}
        ln_steps = {k: sem(f"ln_steps_{k}") for k in "ACFQKN"}
        ln_done = {k: sem(f"ln_done_{k}") for k in "ACFQKN"}
        mask_ready = {j: sem(f"mask_ready_{j}") for j in "AL"}
        res_ready = {j: sem(f"res_ready_{j}") for j in "AL"}
        rows_turned = sem("rows_turned")
        rows_copied = sem("rows_copied")
        hidden_ready = sem("hidden_ready")
        gelus_ready = sem("gelus_ready")
        out_ready = sem("out_ready")
        results_ready = sem("results_ready")
        constants = sem("constants")
        late_weights = sem("late_weights")
        const_steps = sem("const_steps")
        pads_ready = sem("pads_ready")
        halves_ready = sem("halves_ready")
        bias_in = {j: [sem(f"bias_in_{j}{g}") for g in range(NG)] for j in "AC"}
        load = {n: sem(f"load_{n}") for n in ("xT", "cT", "x", "c", "mask_a", "mask_l")}
        stored = sem("stored")

        LN_STEPS = {k: 3 * NT + (2 if k == "F" else 1) for k in "ACFQKN"}
        LN_PARTS = {k: 4 if k in "AN" else 3 for k in "ACFQKN"}

        def wait(eng, semaphore, value):
            if not isinstance(value, int) or value > 0:
                eng.wait_ge(semaphore, value)

        def settle(eng, value):
            if not isinstance(value, int):
                eng.nop(nofuse=True)

        OFFSET = {(s, j, p): d for kind in "CLA" for u in STEPS[kind].values() for s, j, d, p in u}

        def normalised(eng, k, b, plus=0):
            wait(eng, ln_done[k], b * LN_PARTS[k] + (3 + plus))

        def use_of(stage, job, b, part):
            if isinstance(b, int):
                return USES[(stage, job, b, part)]
            b2 = 2 + OFFSET[(stage, job, part)]
            at, first = USES[(stage, job, b2, part)]
            _, second = USES[(stage, job, b2 + 1, part)]
            return at, b * (second - first) + (first - b2 * (second - first))

        def stage_taken(eng, stage, job, b, part):
            at, before = use_of(stage, job, b, part)
            wait(eng, stage_read[at], before + 1)

        def stage_full(eng, stage, job, b, part):
            at, before = use_of(stage, job, b, part)
            wait(eng, stage_filled[at], before + 1)
            return stage_bank[at], stage_read[at]

        def stage_free(eng, stage, job, b, part):
            at, before = use_of(stage, job, b, part)
            wait(eng, stage_read[at], before)
            return stage_bank[at], stage_filled[at]

        PER = 3 * H

        def times(t, per=1, plus=0):
            i, c = t
            return i * (PER * per) + (c * per + plus)

        def copies(t, on_dve):
            i, c = t
            mine = [h for h in range(HG) if (h in COPY_ON_DVE) == on_dve]
            return i * (PER // HG * len(mine)) + (c // HG * len(mine) + sum(h <= c % HG for h in mine))

        def group(t):
            i, c = t
            return i * (PER // HG) + c // HG

        def later(t, n):
            return t[0], t[1] + n

        def run_jobs(eng, warm, step):
            def slot(kind, i, job, b, t0, prev, nxt):
                for h in range(H):
                    step(h, kind, i, job, b, t0, prev, nxt)

            warm("A", 0, (0, 0))
            slot("first", -1, "A", 0, (0, 0), None, ("C", 0, (0, 16)))
            slot("C", 0, "C", 0, (0, 16), ("A", (0, 0)), None)
            slot("L", 0, None, 0, None, ("C", (0, 16)), None)
            warm("A", 1, (0, 32))
            slot("A", 0, "A", 1, (0, 32), None, ("C", 1, (1, 0)))
            with eng.Fori(1, B - 1) as i:
                slot("C", i, "C", i, (i, 0), ("A", (i, -16)), ("L", i - 1, (i, 16)))
                slot("L", i, "L", i - 1, (i, 16), ("C", (i, 0)), ("A", i + 1, (i, 32)))
                slot("A", i, "A", i + 1, (i, 32), ("L", (i, 16)), ("C", i + 1, (i, 48)))
            z = B - 1
            slot("C", z, "C", z, (z, 0), ("A", (z, -16)), ("L", z - 1, (z, 16)))
            slot("L", z, "L", z - 1, (z, 16), ("C", (z, 0)), None)
            slot("A", z, None, 0, None, ("L", (z, 16)), None)
            warm("L", z, (z, 32))
            slot("L", z + 1, "L", z, (z, 32), None, None)
            slot("A", z + 1, None, 0, None, ("L", (z, 32)), None)

        def ahead(h, lead, job, b, t0, nxt):
            if job is None:
                return None
            if h + lead < H:
                return job, b, h + lead, later(t0, h + lead)
            if nxt is None:
                return None
            return nxt[0], nxt[1], h + lead - H, later(nxt[2], h + lead - H)

        block = ctx.enter_context(nc.Block())

        @block.sync
        def _(sp):
            for_w = weights[:, 0:6 * D]
            sp.dma_start(xT[:], t_xT[0]).then_inc(load["xT"], 16)
            sp.dma_start(for_w, t_weights[:, 0:6 * D]).then_inc(constants, 16)
            sp.dma_start(columns[:], t_columns).then_inc(constants, 16)
            sp.dma_start(probsT[:, 0, :, :, :].rearrange("p a b c -> p (a b c)"), t_select).then_inc(constants, 16)
            sp.dma_start(identity[:], t_identity).then_inc(constants, 16)
            sp.dma_start(vectors[:], t_vectors.rearrange("(a n) d -> a n d", a=1)
                         .broadcast_to([P, len(VECTORS), D])).then_inc(constants, 16)
            sp.dma_start(mask_a8[:], t_mask_a[0].rearrange("(t p) k -> p t k", p=P)).then_inc(load["mask_a"], 16)
            sp.dma_start(cT[:], t_cT[0]).then_inc(load["cT"], 16)
            for j, source in (("A", t_bias_a), ("C", t_bias_c)):
                for g in range(NG):
                    for h in range(g * HG, g * HG + HG):
                        sp.dma_start(bias[j][:, h, :, :], source[h].rearrange("(t p) k -> p t k", p=P))\
                            .then_inc(bias_in[j][g], 16)
                if j == "A":
                    sp.dma_start(x_tok[:], t_x[0].rearrange("(t p) d -> p t d", p=P)).then_inc(load["x"], 16)
                    sp.dma_start(weights[:, 6 * D:], t_weights[:, 6 * D:]).then_inc(late_weights, 16)

            def load_batch(i, more):
                if more:
                    wait(sp, split_done["C"], i * 2 + 2)
                    settle(sp, i)
                    sp.dma_start(xT[:], t_xT[i + 1]).then_inc(load["xT"], 16)
                    wait(sp, mask_ready["A"], i + 1)
                    settle(sp, i)
                    sp.dma_start(mask_a8[:], t_mask_a[i + 1].rearrange("(t p) k -> p t k", p=P))\
                        .then_inc(load["mask_a"], 16)
                    wait(sp, res_ready["A"], i + 1)
                    settle(sp, i)
                    sp.dma_start(x_tok[:], t_x[i + 1].rearrange("(t p) d -> p t d", p=P)).then_inc(load["x"], 16)
                    sp.dma_start(cT[:], t_cT[i + 1]).then_inc(load["cT"], 16)
                wait(sp, ln_steps["K"], i * LN_STEPS["K"])
                settle(sp, i)
                sp.dma_start(c_tok[:], t_c[i].rearrange("(t p) d -> p t d", p=P)).then_inc(load["c"], 16)
                wait(sp, mask_ready["L"], i * 1)
                settle(sp, i)
                sp.dma_start(mask_l8[:], t_mask_l[i].rearrange("(t p) k -> p t k", p=P)).then_inc(load["mask_l"], 16)

            load_batch(0, True)
            with sp.Fori(1, B - 1) as i:
                load_batch(i, True)
            load_batch(B - 1, False)
            with sp.Fori(0, B) as b:
                sp.wait_ge(results_ready, b + 1)
                settle(sp, b)
                sp.dma_start(t_out[b].rearrange("(t p) d -> p t d", p=P), x2[:, b, :, :]).then_inc(stored, 16)
            sp.wait_ge(stored, B * 16)

        @block.tensor
        def _(pe):
            def scores(job, b, h, t):
                g, j = h // HG, h % HG
                out = score_bank[t[1] % S_BANKS]
                if h == 0 and job == "A":
                    wait(pe, mask_ready["A"], b + 1)
                wait(pe, maxima_ready, times(t, NT, -NT * (S_BANKS - 1)))
                if job == "A":
                    pe.matmul(out[:], identity16[:], mask_a[:].rearrange("p t k -> p (t k)"), start=True, stop=False,
                              skip_group_check=True)
                for qt in range(NT):
                    last = pe.matmul(out[:, qt * S:(qt + 1) * S],
                                     q_stack[job][32 * j:32 * j + 32, g, qt * P:(qt + 1) * P],
                                     k_stack[job][32 * j:32 * j + 32, g, :], start=job != "A", stop=True,
                                     skip_group_check=True)
                last.then_inc(scores_ready, 1)

            def turn(h, t):
                out = turn_bank[h % T_BANKS]
                before = later(t, -T_BANKS)
                wait(pe, copied_dve if before[1] % HG in COPY_ON_DVE else copied_act,
                     copies(before, before[1] % HG in COPY_ON_DVE))
                wait(pe, exps_ready, times(t, NT, NT))
                for qt in range(NT):
                    for kt in range(NT):
                        last = pe.transpose(out[:, kt * S + qt * P:kt * S + (qt + 1) * P],
                                            probs[:, h % 2, qt, kt * P:(kt + 1) * P], identity[:])
                last.then_inc(turned, 1)

            def weigh_values(job, g, t):
                n = g % 2
                for on_dve in (False, True):
                    wait(pe, copied_dve if on_dve else copied_act, copies(t, on_dve))
                wait(pe, heads_copied, group(t))
                for kt in range(NT):
                    for j in range(HG):
                        last = pe.matmul(head_bank[32 * j:32 * j + 32, n * S:(n + 1) * S],
                                         values[job][:, kt, g * HG + j, :], probsT[:, n, j, kt, :],
                                         start=kt == 0, stop=kt == NT - 1, skip_group_check=True)
                last.then_inc(heads_ready, 1)

            def dense(use, t_fin):
                stage, job, b, part = use
                if stage == "ready":
                    stage_taken(pe, "v", job, b, 0)
                    for n in range(4):
                        stage_taken(pe, "sel", job, b, n)
                if stage in NO_PSUM:
                    return
                if stage == "fin":
                    wait(pe, heads_copied, group(t_fin) + 1)
                elif stage == "oT":
                    if isinstance(b, int) and b == 0:
                        pe.wait_ge(late_weights, 16)
                    stage_taken(pe, "fin", job, b, 3)
                elif stage == "oproj":
                    stage_taken(pe, "oT", job, b, 0)
                elif stage == "qk" and job == "L":
                    stage_taken(pe, "lT", job, b, 0)
                elif stage == "v" and job != "L":
                    source = "xT" if job == "A" else "cT"
                    wait(pe, load[source], b * 16 + 16)
                elif stage == "sel":
                    wait(pe, split_done[job], b * 2 + 2)
                elif stage == "v" and job == "L":
                    stage_taken(pe, "lT", job, b, 0)
                elif stage == "lT":
                    normalised(pe, "K", b)
                    normalised(pe, "Q", b)
                elif stage == "ffT":
                    normalised(pe, "C", b)
                elif stage == "ff1":
                    stage_taken(pe, "ffT", job, b, 0)
                elif stage == "ff2":
                    stage_taken(pe, "ff1", job, b, 0)
                    stage_taken(pe, "ff1", job, b, 1)
                out, filled = stage_free(pe, *use)
                if stage == "fin":
                    for qt in range(NT):
                        last = pe.transpose(out[:, qt * P:(qt + 1) * P], headsT[:, part % 2, qt * P:(qt + 1) * P],
                                            identity[:])
                elif stage == "oT":
                    for qt in range(NT):
                        last = pe.transpose(out[:, qt * P:(qt + 1) * P], attended[job][:, qt, :], identity[:])
                elif stage == "oproj":
                    for qt in range(NT):
                        last = pe.matmul(out[:, qt * D:(qt + 1) * D], attendedT[:, qt * P:(qt + 1) * P],
                                         weight(job + "o"), start=True, stop=True)
                elif stage == "qk":
                    q_in = lT[:, 0, :] if job == "L" else xT[:]
                    k_in = {"A": xT[:], "C": cT[:], "L": lT[:, 1, :]}[job]
                    pe.matmul(out[:, 0:S], weight(job + "q"), q_in, start=True, stop=True)
                    last = pe.matmul(out[:, S:2 * S], weight(job + "k"), k_in, start=True, stop=True)
                elif stage == "sel":
                    side = part // 2
                    for n in range(2):
                        g = part % 2 * 2 + n
                        pe.matmul(out[:, n * S:(n + 1) * S], select[:, 2 * side, g, :], qk_high[:, side, :],
                                  start=True, stop=False)
                        last = pe.matmul(out[:, n * S:(n + 1) * S], select[:, 2 * side + 1, g, :],
                                         qk_low[:, side, :], start=False, stop=True)
                elif stage == "v":
                    source = {"A": xT[:], "C": cT[:], "L": lT[:, 1, :]}[job]
                    for kt in range(NT):
                        last = pe.matmul(out[:, kt * D:(kt + 1) * D], source[:, kt * P:(kt + 1) * P],
                                         weight(job + "v"), start=True, stop=True)
                elif stage == "lT":
                    for n, k in enumerate("QK"):
                        for qt in range(NT):
                            last = pe.transpose(out[:, n * S + qt * P:n * S + (qt + 1) * P], normed[k][:, qt, :],
                                                identity[:])
                elif stage == "ffT":
                    for qt in range(NT):
                        last = pe.transpose(out[:, qt * P:(qt + 1) * P], normed["C"][:, qt, :], identity[:])
                elif stage == "ff1":
                    last = hidden(out, "w1", part)
                elif stage == "ff2":
                    last = from_hidden(out, "w2")
                last.then_inc(filled, 1)

            def hidden(out, w, part):
                for n in range(2):
                    at = W_FF[w] + (2 * part + n) * P
                    last = pe.matmul(out[:, n * S:(n + 1) * S], weights[:, at:at + P], ffT[:], start=True, stop=True)
                return last

            def from_hidden(out, w):
                for qt in range(NT):
                    for c in range(F // P):
                        at = W_FF[w] + c * D
                        last = pe.matmul(out[:, qt * D:(qt + 1) * D], hiddenT[:, c, qt * P:(qt + 1) * P],
                                         weights[:, at:at + D], start=c == 0, stop=c == F // P - 1)
                return last

            def warm(job, b, t0):
                for h in range(LEAD_S):
                    scores(job, b, h, later(t0, h))

            def step(h, kind, i, job, b, t0, prev, nxt):
                far = ahead(h, LEAD_S, job, b, t0, nxt)
                if far:
                    scores(*far)
                if job:
                    turn(h, later(t0, h))
                if h == 1 and prev:
                    weigh_values(prev[0], NG - 1, later(prev[1], H - 1))
                elif h % HG == 1 and h > 1 and job:
                    g = h // HG - 1
                    weigh_values(job, g, later(t0, g * HG + HG - 1))
                for use in stages(kind, i, h):
                    t_fin = later(prev[1], H - 1) if use[0] == "fin" and h == 3 and prev else \
                        later(t0, (h // HG - 1) * HG) if job and h > 3 else None
                    if use[0] == "fin" and t_fin is None:
                        continue
                    dense(use, t_fin)

            pe.wait_ge(constants, 5 * 16)
            pe.wait_ge(const_steps, 4)
            pe.wait_ge(pads_ready, 6)
            for stage, part in PREPARE + [("ready", 0)]:
                dense((stage, "A", 0, part), None)
            run_jobs(pe, warm, step)

            def turn_rows(b):
                normalised(pe, "N", b)
                wait(pe, rows_copied, b)
                for qt in range(NT):
                    last = pe.transpose(score_bank[0][:, qt * P:(qt + 1) * P], normed["A"][:, qt, :], identity[:])
                last.then_inc(rows_turned, 1)

            def feed_forward(b, more):
                wait(pe, rows_copied, b + 1)
                for n in range(2):
                    wait(pe, gelus_ready, b * 2 + (n - 1))
                    hidden(stage_bank[n], "fc1", n).then_inc(hidden_ready, 1)
                if more:
                    turn_rows(b + 1)
                wait(pe, gelus_ready, b * 2 + 2)
                wait(pe, results_ready, b)
                from_hidden(score_bank[1], "fc2").then_inc(out_ready, 1)

            turn_rows(0)
            feed_forward(0, True)
            with pe.Fori(1, B - 1) as b:
                feed_forward(b, True)
            feed_forward(B - 1, False)

        @block.vector
        def _(dve):
            def maximum(job, b, h, t):
                source = score_bank[t[1] % S_BANKS]
                least = neg_max_a if job == "A" else neg_max_cl
                if job in "AC" and isinstance(b, int) and b == 0 and h % HG == 0:
                    dve.wait_ge(bias_in[job][h // HG], HG * 16)
                if job == "L" and h == 0:
                    wait(dve, mask_ready["L"], b + 1)
                wait(dve, scores_ready, times(t, 1, 1))
                wait(dve, exps_ready, times(t, NT, -3 * NT))
                settle(dve, b)
                for qt in range(NT):
                    dve.tensor_tensor_reduce(
                        out=neg_scores[:, h % 4, qt, :], in0=source[:, qt * S:(qt + 1) * S],
                        in1=mask_l[:, qt, :] if job == "L" else bias[job][:, h, qt, :], scale=-1.0, scalar=3.0e38,
                        op0=ALU.add, op1=ALU.min, accum_out=least[:, qt, h:h + 1]).then_inc(maxima_ready, 1)

            def copy_turned(h, t):
                n = (h // HG) % 2
                wait(dve, turned, times(t, 1, 1))
                wait(dve, heads_ready, group(t) - 1)
                dve.tensor_copy(probsT[:, n, h % HG, :, :].rearrange("p a b -> p (a b)"), turn_bank[h % T_BANKS][:])\
                    .then_inc(copied_dve, 1)

            def layer_norm(k, b, source, first=0):
                done, n = ln_steps[k], b * LN_STEPS[k] + first
                for qt in range(NT):
                    dve.bn_stats(out=stats[k][:, qt, :], in_=source(qt)).then_inc(done, 1)
                for qt in range(NT):
                    dve.wait_ge(done, n + 1 + qt)
                    settle(dve, b)
                    dve.bn_aggr(out=mean_var[k][:, qt, :], in_=stats[k][:, qt, :]).then_inc(done, 1)
                dve.wait_ge(done, n + 2 * NT)
                dve.tensor_scalar(mean_var[k][:, :, 1], mean_var[k][:, :, 1], EPS, None, ALU.add).then_inc(done, 1)
                to = normed["A"] if k == "N" else normed[k]
                for qt in range(NT):
                    dve.scalar_tensor_tensor(out=to[:, qt, :], in0=source(qt), scalar=mean_var[k][:, qt, 0:1],
                                             in1=vec(f"ln_{k}_g"), op0=ALU.subtract, op1=ALU.mult).then_inc(done, 1)

            def dense(use, t_fin):
                stage, job, b, part = use
                if stage == "fin":
                    source, read = stage_full(dve, *use)
                    rows = source[:, 0:NT * P].rearrange("p (t j c) -> p t j c", t=NT, j=HG)
                    steps = group(t_fin) * 2
                    if job == "A":
                        dve.scalar_tensor_tensor(out=sums[:], in0=neg_max_a[:, :, part * HG:(part + 1) * HG],
                                                 scalar=-MASKED / 2, in1=rows[:, :, :, HD], op0=ALU.is_lt,
                                                 op1=ALU.mult).then_inc(fin_steps, 1)
                    else:
                        dve.tensor_copy(sums[:], rows[:, :, :, HD]).then_inc(fin_steps, 1)
                    dve.wait_ge(fin_steps, steps + 1)
                    dve.reciprocal(inverse[:], sums[:]).then_inc(fin_steps, 1)
                    dve.wait_ge(fin_steps, steps + 2)
                    to = attended[job][:, :, part * HG * HD:(part + 1) * HG * HD].rearrange("p t (j c) -> p t j c", j=HG)
                    dve.tensor_tensor(to, rows[:, :, :, 0:HD], inverse[:].unsqueeze(3).broadcast_to([P, NT, HG, HD]),
                                      op=ALU.mult).then_inc(read, 1)
                elif stage == "oproj":
                    source, read = stage_full(dve, *use)
                    rows = source[:, 0:NT * D].rearrange("p (t d) -> p t d", t=NT)
                    if job == "L":
                        wait(dve, res_ready["L"], b + 1)
                        dve.tensor_tensor(x2[:, b, :, :], rows, residual["L"][:], op=ALU.add).then_inc(read, 1)
                    else:
                        if job == "A":
                            wait(dve, res_ready["A"], b + 1)
                        else:
                            normalised(dve, "A", b, 1)
                        dve.tensor_tensor(summed[:], rows, residual[job][:], op=ALU.add).then_inc(read, 1)
                        stage_taken(dve, *use)
                        layer_norm(job, b, lambda qt: summed[:, qt, :])
                elif stage == "qk":
                    stage_taken(dve, *use)
                    dve.tensor_copy(qk_high[:], qk_plain[:]).then_inc(split_done[job], 1)
                    dve.wait_ge(split_done[job], b * 2 + 1)
                    dve.tensor_tensor(qk_low[:], qk_plain[:], qk_high[:].bitcast(f32), op=ALU.subtract)\
                        .then_inc(split_done[job], 1)
                elif stage == "sel" and part % 2 == 1:
                    source, read = stage_full(dve, *use)
                    to = (q_stack if part // 2 == 0 else k_stack)[job]
                    dve.tensor_copy(to[:, 2:4, :].rearrange("p g s -> p (g s)"), source[:]).then_inc(read, 1)
                elif stage == "v" and job != "L":
                    source, read = stage_full(dve, *use)
                    dve.tensor_tensor(values[job][:, :, :, 0:HD],
                                      source[:, 0:NT * D].rearrange("p (t h c) -> p t h c", t=NT, h=H),
                                      vec2(job + "v_b").rearrange("p t (h c) -> p t h c", h=H), op=ALU.add)\
                        .then_inc(read, 1)
                elif stage == "ff2":
                    source, read = stage_full(dve, *use)
                    rows = source[:, 0:NT * D].rearrange("p (t d) -> p t d", t=NT)
                    dve.tensor_tensor(ff_out[:], rows, vec2("ff_b2"), op=ALU.add).then_inc(read, 1)
                    stage_taken(dve, *use)
                    normalised(dve, "C", b)
                    dve.scalar_tensor_tensor(out=summed[:], in0=ff_out[:], scalar=0.0, in1=normed["C"][:],
                                             op0=ALU.max, op1=ALU.add).then_inc(ln_steps["F"], 1)
                    dve.wait_ge(ln_steps["F"], b * LN_STEPS["F"] + 1)
                    wait(dve, res_ready["L"], b * 1)
                    layer_norm("F", b, lambda qt: summed[:, qt, :], 1)
                elif stage == "lnQ":
                    normalised(dve, "F", b)
                    layer_norm("Q", b, lambda qt: normed["F"][:, qt, :])
                elif stage == "lnK":
                    dve.wait_ge(load["c"], b * 16 + 16)
                    layer_norm("K", b, lambda qt: c_tok[:, qt, :])

            def warm(job, b, t0):
                for h in range(LEAD_M):
                    maximum(job, b, h, later(t0, h))

            def step(h, kind, i, job, b, t0, prev, nxt):
                far = ahead(h, LEAD_M, job, b, t0, nxt)
                if far:
                    maximum(*far)
                if job and h % HG in COPY_ON_DVE:
                    copy_turned(h, later(t0, h))
                for use in stages(kind, i, h):
                    t_fin = later(prev[1], H - 1) if use[0] == "fin" and h == 3 and prev else \
                        later(t0, (h // HG - 1) * HG) if job and h > 3 else None
                    if use[0] == "fin" and t_fin is None:
                        continue
                    dense(use, t_fin)

            dve.wait_ge(constants, 5 * 16)
            dve.tensor_copy(select[:].rearrange("p a g c -> p (a g c)"),
                            probsT[:, 0, :, :, :].rearrange("p a b c -> p (a b c)")).then_inc(const_steps, 1)
            dve.tensor_copy(identity16[:], identity[:]).then_inc(const_steps, 1)
            for job in "AC":
                at = COLUMN[job + "q"]
                dve.tensor_scalar(columns[:, at:at + 1], columns[:, at:at + 1], SCALE[job], None, ALU.mult)\
                    .then_inc(const_steps, 1)
            for stage, part in PREPARE:
                dense((stage, "A", 0, part), None)
            run_jobs(dve, warm, step)

            def norm_rows(b):
                wait(dve, rows_copied, b)
                layer_norm("N", b, lambda qt: x2[:, b, qt, :])

            def add_result(b):
                normalised(dve, "N", b, 1)
                wait(dve, out_ready, b + 1)
                dve.tensor_tensor(x2[:, b, :, :], score_bank[1][:, 0:NT * D].rearrange("p (t d) -> p t d", t=NT),
                                  residual["A"][:], op=ALU.add).then_inc(results_ready, 1)

            stage_taken(dve, "oproj", "L", B - 1, 0)
            norm_rows(0)
            norm_rows(1)
            add_result(0)
            with dve.Fori(1, B - 1) as b:
                norm_rows(b + 1)
                add_result(b)
            add_result(B - 1)

        @block.scalar
        def _(act):
            def exponentials(h, t, job):
                least = neg_max_a if job == "A" else neg_max_cl
                wait(act, turned, times(t, 1, -1))
                for qt in range(NT):
                    wait(act, maxima_ready, times(t, NT, qt + 1))
                    act.activation(probs[:, h % 2, qt, :], neg_scores[:, h % 4, qt, :], ACT.Exp,
                                   bias=least[:, qt, h:h + 1], scale=-1.0).then_inc(exps_ready, 1)

            def copy_turned(h, t):
                n = (h // HG) % 2
                wait(act, turned, times(t, 1, 1))
                wait(act, heads_ready, group(t) - 1)
                act.activation(probsT[:, n, h % HG, :, :].rearrange("p a b -> p (a b)"), turn_bank[h % T_BANKS][:],
                               ACT.Copy).then_inc(copied_act, 1)

            def copy_heads(t, g):
                n = g % 2
                wait(act, heads_ready, group(t) + 1)
                act.activation(headsT[:, n, :], head_bank[:, n * S:(n + 1) * S], ACT.Copy).then_inc(heads_copied, 1)

            def dense(use):
                stage, job, b, part = use
                if stage == "qk":
                    source, read = stage_full(act, *use)
                    if job == "L":
                        act.activation(qk_plain[:, 0, :], source[:, 0:S], ACT.Copy, scale=SCALE[job])
                        act.activation(qk_plain[:, 1, :], source[:, S:2 * S], ACT.Copy).then_inc(read, 1)
                    else:
                        at = COLUMN[job + "q"]
                        act.activation(qk_plain[:, 0, :], source[:, 0:S], ACT.Identity, bias=columns[:, at:at + 1],
                                       scale=SCALE[job])
                        act.activation(qk_plain[:, 1, :], source[:, S:2 * S], ACT.Identity,
                                       bias=columns[:, at + 1:at + 2]).then_inc(read, 1)
                elif stage == "sel" and part % 2 == 0:
                    source, read = stage_full(act, *use)
                    to = (q_stack if part // 2 == 0 else k_stack)[job]
                    act.activation(to[:, 0:2, :].rearrange("p g s -> p (g s)"), source[:], ACT.Copy).then_inc(read, 1)
                elif stage == "v" and job == "L":
                    source, read = stage_full(act, *use)
                    act.activation(values[job][:, :, :, 0:HD],
                                   source[:, 0:NT * D].rearrange("p (t h c) -> p t h c", t=NT, h=H), ACT.Copy)\
                        .then_inc(read, 1)
                elif stage in ("oT", "ffT"):
                    source, read = stage_full(act, *use)
                    act.activation((attendedT if stage == "oT" else ffT)[:], source[:, 0:S], ACT.Copy).then_inc(read, 1)
                elif stage == "lT":
                    source, read = stage_full(act, *use)
                    act.activation(lT[:].rearrange("p a s -> p (a s)"), source[:], ACT.Copy).then_inc(read, 1)
                elif stage == "ff1":
                    source, read = stage_full(act, *use)
                    hidden(source, part, ACT.Relu, "b1").then_inc(read, 1)

            def hidden(source, part, func, bias_name):
                for n in range(2):
                    c = 2 * part + n
                    at = COLUMN[bias_name] + c
                    last = act.activation(hiddenT[:, c, :], source[:, n * S:(n + 1) * S], func,
                                          bias=columns[:, at:at + 1])
                return last

            def warm(job, b, t0):
                exponentials(0, t0, job)

            def step(h, kind, i, job, b, t0, prev, nxt):
                far = ahead(h, LEAD_E, job, b, t0, nxt)
                if far:
                    exponentials(far[2], far[3], far[0])
                if job and h % HG not in COPY_ON_DVE:
                    copy_turned(h, later(t0, h))
                if h == 2 and prev:
                    copy_heads(later(prev[1], H - 1), NG - 1)
                elif h % HG == 2 and h > 2 and job:
                    copy_heads(later(t0, (h // HG - 1) * HG), h // HG - 1)
                for use in stages(kind, i, h):
                    dense(use)

            act.wait_ge(constants, 5 * 16)
            act.wait_ge(const_steps, 4)
            for stage, part in PREPARE:
                dense((stage, "A", 0, part))
            run_jobs(act, warm, step)

            def copy_rows(b):
                wait(act, rows_turned, b + 1)
                act.activation(ffT[:], score_bank[0][:, 0:S], ACT.Copy).then_inc(rows_copied, 1)

            def gelus(b):
                for n in range(2):
                    wait(act, hidden_ready, b * 2 + (n + 1))
                    hidden(stage_bank[n], n, ACT.Gelu, "fc1_b").then_inc(gelus_ready, 1)

            copy_rows(0)
            gelus(0)
            with act.Fori(1, B) as b:
                copy_rows(b)
                gelus(b)

        @block.gpsimd
        def _(pool):
            def normalise(k, b):
                to = normed["A"] if k == "N" else normed[k]
                n = b * LN_PARTS[k]
                wait(pool, ln_steps[k], b * LN_STEPS[k] + (LN_STEPS[k] - NT))
                pool.tensor_tensor(rstd[k][:], mean_var[k][:, :, 1], minus_half[:], op=ALU.pow).then_inc(ln_done[k], 1)
                wait(pool, ln_done[k], n + 1)
                wait(pool, ln_steps[k], b * LN_STEPS[k] + LN_STEPS[k])
                pool.tensor_tensor(to[:], to[:], rstd[k][:].unsqueeze(2).broadcast_to([P, NT, D]), op=ALU.mult)\
                    .then_inc(ln_done[k], 1)
                wait(pool, ln_done[k], n + 2)
                pool.tensor_tensor(to[:], to[:], vec2(f"ln_{k}_b"), op=ALU.add).then_inc(ln_done[k], 1)

            def dense(use, t_before):
                stage, job, b, part = use
                if stage == "maskA":
                    wait(pool, load["mask_a"], b * 16 + 16)
                    if t_before:
                        wait(pool, scores_ready, times(t_before))
                    settle(pool, b)
                    pool.tensor_scalar(mask_a[:], mask_a8[:], MASKED, None, ALU.mult).then_inc(mask_ready["A"], 1)
                elif stage == "maskL":
                    wait(pool, load["mask_l"], b * 16 + 16)
                    if t_before:
                        wait(pool, maxima_ready, times(t_before, NT))
                    settle(pool, b)
                    pool.tensor_scalar(mask_l[:], mask_l8[:], MASKED, None, ALU.mult).then_inc(mask_ready["L"], 1)
                elif stage == "resA":
                    wait(pool, load["x"], b * 16 + 16)
                    wait(pool, ln_steps["A"], b * LN_STEPS["A"] - 3 * NT)
                    pool.tensor_tensor(residual["A"][:], x_tok[:], vec2("Ao_b"), op=ALU.add).then_inc(res_ready["A"], 1)
                elif stage == "oproj" and job in "AC":
                    normalise(job, b)
                    if job == "A":
                        normalised(pool, "A", b)
                        pool.tensor_tensor(residual["C"][:], normed["A"][:], vec2("Co_b"), op=ALU.add)\
                            .then_inc(ln_done["A"], 1)
                elif stage == "ff2":
                    normalise("F", b)
                elif stage in ("lnQ", "lnK"):
                    normalise(job, b)
                elif stage == "resL":
                    if not isinstance(b, int) or b > 0:
                        stage_taken(pool, "oproj", "L", b - 1, 0)
                    normalised(pool, "F", b)
                    pool.tensor_tensor(residual["L"][:], normed["F"][:], vec2("Lo_b"), op=ALU.add)\
                        .then_inc(res_ready["L"], 1)

            def step(h, kind, i, job, b, t0, prev, nxt):
                for use in stages(kind, i, h):
                    dense(use, later(prev[1], H) if prev else None)

            pool.memset(minus_half[:], -0.5).then_inc(halves_ready, 1)
            pool.wait_ge(halves_ready, 1)
            for n, job in enumerate("ACL"):
                pool.memset(values[job][:], 0.0).then_inc(pads_ready, 1)
                pool.wait_ge(pads_ready, 2 * n + 1)
                pool.memset(values[job][:, :, :, HD:HD + 1], 1.0).then_inc(pads_ready, 1)
            dense(("maskA", "A", 0, 0), None)
            pool.wait_ge(constants, 5 * 16)
            dense(("resA", "A", 0, 0), None)
            run_jobs(pool, lambda *_: None, step)

            def rows(b):
                normalise("N", b)
                wait(pool, results_ready, b)
                pool.tensor_tensor(residual["A"][:], x2[:, b, :, :], vec2("fc2_b"), op=ALU.add)\
                    .then_inc(ln_done["N"], 1)

            rows(0)
            with pool.Fori(1, B) as b:
                rows(b)


def selections():
    import numpy as np
    m = np.zeros((P, PARTS, NG, P), np.float32)
    for g in range(NG):
        for j in range(HG):
            for part in range(PARTS):
                for d in range(HD):
                    row, col = (g * HG + j) * HD + d, 32 * j + HD * part + d
                    m[row, part // 2, g, col] = 1.0
                    m[row, 2 + part % 2, g, col] = 1.0
    return m.reshape(P, PARTS * NG * P)


def kernel(**inputs):
    import numpy as np
    import concourse.bacc as bacc
    from concourse.bass_utils import run_bass_kernel_spmd

    a = {k: np.asarray(v) for k, v in inputs.items()}
    l0, l1 = "L0_xattn_", "L1_xattn_"
    kv = a[l1 + "kv_w"]
    square = [a[l0 + "sa_wq"], a[l0 + "sa_wk"], a[l0 + "sa_wv"], a[l0 + "ca_wq"], a[l0 + "ca_wk"], a[l0 + "ca_wv"],
              a[l0 + "sa_wo"], a[l0 + "ca_wo"], a[l1 + "q_w"], kv[:, :D], kv[:, D:], a[l1 + "proj_w"]]

    def by_rows(w):
        return w.reshape(F // P, P, D).transpose(1, 0, 2).reshape(P, F)

    weights = np.concatenate(square + [a[l0 + "ff_w1"], by_rows(a[l0 + "ff_w2"]), a[l1 + "fc1_w"],
                                       by_rows(a[l1 + "fc2_w"])], axis=1)
    columns = np.concatenate([a[l0 + n].reshape(-1, P) for n in ("sa_bq", "sa_bk", "ca_bq", "ca_bk", "ff_b1")]
                             + [a[l1 + "fc1_b"].reshape(-1, P)], axis=0).T
    names = {"Av_b": l0 + "sa_bv", "Cv_b": l0 + "ca_bv", "Ao_b": l0 + "sa_bo", "Co_b": l0 + "ca_bo",
             "Lo_b": l1 + "proj_b", "ln_A_g": l0 + "sa_g", "ln_A_b": l0 + "sa_b", "ln_C_g": l0 + "ca_g",
             "ln_C_b": l0 + "ca_b", "ln_F_g": l0 + "ff_g", "ln_F_b": l0 + "ff_b", "ln_Q_g": l1 + "qn_w",
             "ln_Q_b": l1 + "qn_b", "ln_K_g": l1 + "cn_w", "ln_K_b": l1 + "cn_b", "ln_N_g": l1 + "n2_w",
             "ln_N_b": l1 + "n2_b", "ff_b2": l0 + "ff_b2", "fc2_b": l1 + "fc2_b"}
    arrays = {
        "x": a["x"], "x_turned": a["x"].transpose(0, 2, 1),
        "ctx": a["ctx_1024"], "ctx_turned": a["ctx_1024"].transpose(0, 2, 1),
        "mask_self": a["mask_BxSxS2_bk1"], "mask_cross": a["mask_BxSxS2_bk0"],
        "bias_self": a["fside_1x16xSxS2_0"][0], "bias_cross": a[l0 + "attn_2d_bias"][0],
        "weights": weights, "columns": columns, "vectors": np.stack([a[names[n]] for n in VECTORS]),
        "selections": selections(), "identity": np.eye(P, dtype=np.float32),
    }
    nc = bacc.Bacc("TRN2", target_bir_lowering=False, num_devices=1)
    args = []
    for name in arrays:
        arrays[name] = np.ascontiguousarray(arrays[name])
        args.append(nc.dram_tensor("in_" + name, arrays[name].shape, mybir.dt.from_np(arrays[name].dtype),
                                   kind="ExternalInput").ap())
    args.append(nc.dram_tensor("out", (B, S, D), mybir.dt.float32, kind="ExternalOutput").ap())
    two_layers(nc, *args)
    r = run_bass_kernel_spmd(nc, [{"in_" + n: v for n, v in arrays.items()}], core_ids=[0])
    return r.results[0]["out"]
```

```python
import concourse.bass as bass
from concourse import mybir
from contextlib import ExitStack


B, S, D, H, F = 8, 256, 128, 16, 512
P = 128
HD = D // H
NT = S // P
HG = 4
NG = H // HG
PARTS = 4
EPS = 1e-5
MASKED = -2.0 ** 100
SCALE = {"A": float(D) ** -0.5, "C": float(D) ** -0.5, "L": float(HD) ** -0.5}

WEIGHTS = ["Aq", "Ak", "Av", "Cq", "Ck", "Cv", "Ao", "Co", "Lq", "Lk", "Lv", "Lo"]
W_FF = {"w1": 12 * D, "w2": 12 * D + F, "fc1": 12 * D + 2 * F, "fc2": 12 * D + 3 * F}
W_COLS = 12 * D + 4 * F
COLUMN = {"Aq": 0, "Ak": 1, "Cq": 2, "Ck": 3, "b1": 4, "fc1_b": 8}
N_COLUMN = 12
VECTORS = ["Av_b", "Cv_b", "Ao_b", "Co_b", "Lo_b", "ln_A_g", "ln_A_b", "ln_C_g", "ln_C_b", "ln_F_g", "ln_F_b",
           "ln_Q_g", "ln_Q_b", "ln_K_g", "ln_K_b", "ln_N_g", "ln_N_b", "ff_b2", "fc2_b"]

LEAD_S, LEAD_M, LEAD_E = 4, 3, 2
S_BANKS, T_BANKS = 3, 2
N_SCORES, N_PROBS = 4, 3
COPY_ON_DVE = (1, 3)

STEPS = {
    "first": {2: [("qk", "C", 1, 0)], 3: [("split", "C", 1, 0)], 4: [("v", "C", 1, 0)], 6: [("sel", "C", 1, 0)],
              7: [("sel", "C", 1, 1)], 8: [("sel", "C", 1, 2)], 9: [("sel", "C", 1, 3)], 12: [("fin", "A", 1, 0)]},
    "C": {0: [("qk", "A", 1, 0)], 1: [("split", "A", 1, 0)], 2: [("v", "A", 1, 0)], 4: [("fin", "A", 0, 1)],
          5: [("sel", "A", 1, 0)], 6: [("oT", "A", 0, 0)], 7: [("sel", "A", 1, 1)], 8: [("oproj", "A", 0, 0)],
          9: [("sel", "A", 1, 2)], 10: [("sel", "A", 1, 3)], 12: [("fin", "C", 0, 0), ("maskA", "A", 1, 0)]},
    "L": {0: [("qk", "C", 1, 0)], 1: [("split", "C", 1, 0)], 2: [("v", "C", 1, 0)], 4: [("fin", "C", 0, 1)],
          5: [("sel", "C", 1, 0)], 6: [("oT", "C", 0, 0), ("resA", "A", 1, 0)], 7: [("sel", "C", 1, 1)],
          8: [("oproj", "C", 0, 0)], 9: [("sel", "C", 1, 2)], 10: [("sel", "C", 1, 3)], 11: [("ffT", "F", 0, 0)],
          12: [("fin", "L", -1, 0)], 13: [("ff1", "F", 0, 0)], 14: [("ff1", "F", 0, 1)]},
    "A": {0: [("ff2", "F", 0, 0)], 1: [("lnK", "K", 0, 0)], 3: [("lnQ", "Q", 0, 0)], 4: [("fin", "L", -1, 1)],
          6: [("oT", "L", -1, 0)], 7: [("lT", "L", 0, 0)], 8: [("oproj", "L", -1, 0)], 9: [("qk", "L", 0, 0)],
          10: [("split", "L", 0, 0), ("v", "L", 0, 0), ("resL", "L", 0, 0)], 12: [("fin", "A", 1, 0), ("maskL", "L", 0, 0)],
          11: [("sel", "L", 0, 0)], 13: [("sel", "L", 0, 1)], 14: [("sel", "L", 0, 2)], 15: [("sel", "L", 0, 3)]},
}


def both(more):
    table = {h: list(use) for h, use in more.items()}
    for n, kind in enumerate("LA"):
        for h in range(H):
            for use in STEPS[kind].get(h, []):
                if use[0] not in ("fin", "oT", "oproj", "resL", "maskL") or use[1] == "C":
                    table.setdefault(min((n * H + h + 2) // 2, H - 1), []).append(use)
    return table


STEPS["start"] = both({12: [("fin", "A", 1, 0), ("resL", "L", 0, 0), ("maskL", "L", 0, 0)]})
STEPS["end"] = both({8: [("maskL", "L", 0, 0)], 12: [("fin", "L", -1, 0)]})
STEPS["last"] = {4: [("fin", "L", -1, 1)], 6: [("oT", "L", -1, 0)], 8: [("oproj", "L", -1, 0)],
                 10: [("resL", "L", 0, 0)], 12: [("fin", "L", 0, 0)]}
STEPS["drain"] = {4: [("fin", "L", 0, 1)], 6: [("oT", "L", 0, 0)], 8: [("oproj", "L", 0, 0)]}
TICK_AT = {1: 0, 2: 1, 3: 2, 5: 3, 7: 4, 9: 5, 11: 6, 13: 7, 14: 8, 15: 9}
CROWDED = ("start", "end")
NO_PSUM = ("maskA", "maskL", "resA", "resL", "lnK", "lnQ", "split")
PREPARE = [("qk", 0), ("split", 0), ("v", 0), ("sel", 0), ("sel", 1), ("sel", 2), ("sel", 3)]


def stages(kind, i, h):
    known = isinstance(i, int)
    return [(s, j, i + d, p) for s, j, d, p in STEPS[kind].get(h, []) if not known or 0 <= i + d < B]


def number_stage_banks():
    found, before = {}, [0, 0]

    def segment(uses):
        for n, use in enumerate(uses):
            found[use] = (n % 2, before[n % 2])
            before[n % 2] += 1

    def of(kind, i):
        return [u for h in range(H) for u in stages(kind, i, h) if u[0] not in NO_PSUM]

    segment([(s, "A", 0, p) for s, p in PREPARE if s not in NO_PSUM] + of("first", -1) + of("C", 0) + of("start", 0))
    for i in range(1, B - 1):
        segment(of("C", i) + of("L", i) + of("A", i))
    segment(of("C", B - 1) + of("end", B - 1) + of("last", B - 1) + of("drain", B - 1))
    return found


USES = number_stage_banks()


def two_layers(nc: bass.Bass, t_x, t_xT, t_c, t_cT, t_mask_a, t_mask_l, t_bias_a, t_bias_c, t_weights, t_columns,
               t_vectors, t_select, t_identity, t_out):
    f32, f32r, bf16, u8 = mybir.dt.float32, mybir.dt.float32r, mybir.dt.bfloat16, mybir.dt.uint8
    ALU, ACT = mybir.AluOpType, mybir.ActivationFunctionType

    with ExitStack() as ctx:
        def sb(name, shape, dt=f32):
            return ctx.enter_context(nc.sbuf_tensor(name, shape, dt))

        def bank(name):
            return ctx.enter_context(nc.psum_tensor(name, [P, 512], f32))

        def sem(name):
            return ctx.enter_context(nc.semaphore(name))

        bias = {"A": sb("bias_a", [P, H, NT, S]), "C": sb("bias_c", [P, H, NT, S])}
        q_stack = {j: sb(f"q_stack_{j}", [P, NG, S], f32r) for j in "ACL"}
        k_stack = {j: sb(f"k_stack_{j}", [P, NG, S], f32r) for j in "ACL"}
        values = {j: sb(f"values_{j}", [P, NT, H, HD + 1]) for j in "ACL"}
        neg_scores = sb("neg_scores", [P, N_SCORES, NT, S])
        neg_max_a = sb("neg_max_a", [P, NT, H])
        neg_max_cl = sb("neg_max_cl", [P, NT, H])
        probs = sb("probs", [P, N_PROBS, NT, S])
        probsT = sb("probsT", [P, 2, HG, NT, S])
        headsT = sb("headsT", [P, NG, S])
        sums = sb("sums", [P, NT, H // 2])
        inverse = sb("inverse", [P, NT, H // 2])
        attended = {j: sb(f"attended_{j}", [P, NT, D]) for j in "ACL"}
        attendedT = sb("attendedT", [P, S])
        qk_plain = sb("qk_plain", [P, 2, S])
        qk_high = sb("qk_high", [P, 2, S], f32r)
        qk_low = sb("qk_low", [P, 2, S], f32r)
        weights = sb("weights", [P, W_COLS])
        columns = sb("columns", [P, N_COLUMN])
        vectors = sb("vectors", [P, len(VECTORS), D])
        select = sb("select", [P, PARTS, NG, P], f32r)
        identity = sb("identity", [P, P])
        identity16 = sb("identity16", [P, P], bf16)
        xT, cT = sb("xT", [P, S]), sb("cT", [P, S])
        x_tok, c_tok = sb("x_tok", [P, NT, D]), sb("c_tok", [P, NT, D])
        mask_a8, mask_l8 = sb("mask_a8", [P, NT, S], u8), sb("mask_l8", [P, NT, S], u8)
        mask_a, mask_l = sb("mask_a", [P, NT, S], bf16), sb("mask_l", [P, NT, S], bf16)
        masks = {"A": mask_a, "L": mask_l}
        residual = {j: sb(f"residual_{j}", [P, NT, D]) for j in "ACL"}
        summed = sb("summed", [P, NT, D])
        ff_out = sb("ff_out", [P, NT, D])
        normed = {k: sb(f"normed_{k}", [P, NT, D]) for k in "ACFQK"}
        stats = {k: sb(f"stats_{k}", [P, NT, 6]) for k in "ACFQKN"}
        minus_half = sb("minus_half", [P, NT])
        mean_var = {k: sb(f"mean_var_{k}", [P, NT, 2]) for k in "ACFQKN"}
        rstd = {k: sb(f"rstd_{k}", [P, NT]) for k in "ACFQKN"}
        ffT = sb("ffT", [P, S])
        hiddenT = sb("hiddenT", [P, 2, F // P, S])
        lT = sb("lT", [P, 2, S])
        x2 = sb("x2", [P, B, NT, D])

        def vec(name):
            return vectors[:, VECTORS.index(name), :]

        def vec2(name):
            return vectors[:, VECTORS.index(name):VECTORS.index(name) + 1, :].broadcast_to([P, NT, D])

        def weight(name):
            n = WEIGHTS.index(name)
            return weights[:, n * D:(n + 1) * D]

        score_bank = [bank(f"score_bank{n}") for n in range(S_BANKS)]
        turn_bank = [bank(f"turn_bank{n}") for n in range(T_BANKS)]
        head_bank = bank("head_bank")
        stage_bank = [bank(f"stage_bank{n}") for n in range(2)]

        scores_ready = sem("scores_ready")
        maxima_ready = sem("maxima_ready")
        exps_ready = sem("exps_ready")
        turned = sem("turned")
        copied_act = sem("copied_act")
        copied_dve = sem("copied_dve")
        heads_ready = sem("heads_ready")
        heads_copied = sem("heads_copied")
        fin_steps = sem("fin_steps")
        stage_filled = [sem(f"stage_filled{n}") for n in range(2)]
        stage_read = [sem(f"stage_read{n}") for n in range(2)]
        split_done = {j: sem(f"split_done_{j}") for j in "ACL"}
        ln_steps = {k: sem(f"ln_steps_{k}") for k in "ACFQKN"}
        ln_done = {k: sem(f"ln_done_{k}") for k in "ACFQKN"}
        mask_ready = {j: sem(f"mask_ready_{j}") for j in "AL"}
        res_ready = {j: sem(f"res_ready_{j}") for j in "AL"}
        rows_turned = sem("rows_turned")
        rows_copied = sem("rows_copied")
        hidden_ready = sem("hidden_ready")
        gelus_ready = sem("gelus_ready")
        out_ready = sem("out_ready")
        results_ready = sem("results_ready")
        constants = sem("constants")
        late_weights = sem("late_weights")
        const_steps = sem("const_steps")
        pads_ready = sem("pads_ready")
        halves_ready = sem("halves_ready")
        bias_in = {j: [sem(f"bias_in_{j}{g}") for g in range(NG)] for j in "AC"}
        load = {n: sem(f"load_{n}") for n in ("xT", "cT", "x", "c", "mask_a", "mask_l")}
        stored = sem("stored")

        LN_STEPS = {k: 3 * NT + (2 if k == "F" else 1) for k in "ACFQK"} | {"N": 4 * NT + 1}
        LN_PARTS = {k: 4 if k == "A" else 3 for k in "ACFQK"} | {"N": 2}

        def wait(eng, semaphore, value):
            if not isinstance(value, int) or value > 0:
                eng.wait_ge(semaphore, value)

        def settle(eng, value):
            if not isinstance(value, int):
                eng.nop(nofuse=True)

        OFFSET = {(s, j, p): d for kind in "CLA" for u in STEPS[kind].values() for s, j, d, p in u}

        def normalised(eng, k, b, plus=0):
            wait(eng, ln_done[k], b * LN_PARTS[k] + (3 + plus))

        def use_of(stage, job, b, part):
            if isinstance(b, int):
                return USES[(stage, job, b, part)]
            b2 = 2 + OFFSET[(stage, job, part)]
            at, first = USES[(stage, job, b2, part)]
            _, second = USES[(stage, job, b2 + 1, part)]
            return at, b * (second - first) + (first - b2 * (second - first))

        def stage_taken(eng, stage, job, b, part):
            at, before = use_of(stage, job, b, part)
            wait(eng, stage_read[at], before + 1)

        def stage_full(eng, stage, job, b, part):
            at, before = use_of(stage, job, b, part)
            wait(eng, stage_filled[at], before + 1)
            return stage_bank[at], stage_read[at]

        def stage_free(eng, stage, job, b, part):
            at, before = use_of(stage, job, b, part)
            wait(eng, stage_read[at], before)
            return stage_bank[at], stage_filled[at]

        PER = 3 * H

        def times(t, per=1, plus=0):
            i, c = t
            return i * (PER * per) + (c * per + plus)

        def copies(t, on_dve):
            i, c = t
            mine = [h for h in range(HG) if (h in COPY_ON_DVE) == on_dve]
            return i * (PER // HG * len(mine)) + (c // HG * len(mine) + sum(h <= c % HG for h in mine))

        def group(t):
            i, c = t
            return i * (PER // HG) + c // HG

        def fins_before(t):
            i, c = t
            return i * (PER // (H // 2)) + c // (H // 2)

        def later(t, n):
            return t[0], t[1] + n

        def run_jobs(eng, warm, step, tick):
            def slot(kind, i, job, b, t0, prev, nxt):
                for h in range(H):
                    step(h, kind, i, job, b, t0, prev, nxt)

            warm("A", 0, (0, 0))
            slot("first", -1, "A", 0, (0, 0), None, ("C", 0, (0, 16)))
            slot("C", 0, "C", 0, (0, H), ("A", 0, (0, 0)), ("A", 1, (0, 2 * H)))
            slot("start", 0, "A", 1, (0, 2 * H), ("C", 0, (0, H)), ("C", 1, (1, 0)))
            with eng.Fori(1, B - 1) as i:
                slot("C", i, "C", i, (i, 0), ("A", i, (i, -H)), ("L", i - 1, (i, H)))
                slot("L", i, "L", i - 1, (i, H), ("C", i, (i, 0)), ("A", i + 1, (i, 2 * H)))
                slot("A", i, "A", i + 1, (i, 2 * H), ("L", i - 1, (i, H)), ("C", i + 1, (i, 3 * H)))
            z = B - 1
            slot("C", z, "C", z, (z, 0), ("A", z, (z, -H)), ("L", z - 1, (z, H)))
            slot("end", z, "L", z - 1, (z, H), ("C", z, (z, 0)), None)
            warm("L", z, (z, 2 * H))
            slot("last", z, "L", z, (z, 2 * H), ("L", z - 1, (z, H)), None)
            for h in range(H):
                step(h, "drain", z, None, 0, None, ("L", z, (z, 2 * H)), None)
                if h in TICK_AT:
                    tick(TICK_AT[h])

        def ahead(h, lead, job, b, t0, nxt):
            if job is None:
                return None
            if h + lead < H:
                return job, b, h + lead, later(t0, h + lead)
            if nxt is None:
                return None
            return nxt[0], nxt[1], h + lead - H, later(nxt[2], h + lead - H)

        def own(job, b):
            return "A" if job == "L" and isinstance(b, int) and b == B - 1 else job

        def last_head(use, t0, prev):
            if use[0] != "fin":
                return None
            return later(t0, H // 2 - 1) if use[3] == 0 else later(prev[2], H - 1)

        block = ctx.enter_context(nc.Block())

        @block.sync
        def _(sp):
            for_w = weights[:, 0:6 * D]
            sp.dma_start(xT[:], t_xT[0]).then_inc(load["xT"], 16)
            sp.dma_start(for_w, t_weights[:, 0:6 * D]).then_inc(constants, 16)
            sp.dma_start(columns[:], t_columns).then_inc(constants, 16)
            sp.dma_start(probsT[:, 0, :, :, :].rearrange("p a b c -> p (a b c)"), t_select).then_inc(constants, 16)
            sp.dma_start(identity[:], t_identity).then_inc(constants, 16)
            sp.dma_start(vectors[:], t_vectors.rearrange("(a n) d -> a n d", a=1)
                         .broadcast_to([P, len(VECTORS), D])).then_inc(constants, 16)
            sp.dma_start(mask_a8[:], t_mask_a[0].rearrange("(t p) k -> p t k", p=P)).then_inc(load["mask_a"], 16)
            sp.dma_start(cT[:], t_cT[0]).then_inc(load["cT"], 16)
            for j, source in (("A", t_bias_a), ("C", t_bias_c)):
                for g in range(NG):
                    for h in range(g * HG, g * HG + HG):
                        sp.dma_start(bias[j][:, h, :, :], source[h].rearrange("(t p) k -> p t k", p=P))\
                            .then_inc(bias_in[j][g], 16)
                if j == "A":
                    sp.dma_start(x_tok[:], t_x[0].rearrange("(t p) d -> p t d", p=P)).then_inc(load["x"], 16)
                    sp.dma_start(weights[:, 6 * D:], t_weights[:, 6 * D:]).then_inc(late_weights, 16)

            def load_batch(i, more):
                if more:
                    wait(sp, split_done["C"], i * 2 + 2)
                    settle(sp, i)
                    sp.dma_start(xT[:], t_xT[i + 1]).then_inc(load["xT"], 16)
                    wait(sp, mask_ready["A"], i + 1)
                    settle(sp, i)
                    sp.dma_start(mask_a8[:], t_mask_a[i + 1].rearrange("(t p) k -> p t k", p=P))\
                        .then_inc(load["mask_a"], 16)
                    wait(sp, res_ready["A"], i + 1)
                    settle(sp, i)
                    sp.dma_start(x_tok[:], t_x[i + 1].rearrange("(t p) d -> p t d", p=P)).then_inc(load["x"], 16)
                    wait(sp, heads_ready, group((i, 0) if not isinstance(i, int) or i > 0 else (0, H)) + 1)
                    settle(sp, i)
                    sp.dma_start(cT[:], t_cT[i + 1]).then_inc(load["cT"], 16)
                wait(sp, ln_steps["K"], i * LN_STEPS["K"])
                settle(sp, i)
                sp.dma_start(c_tok[:], t_c[i].rearrange("(t p) d -> p t d", p=P)).then_inc(load["c"], 16)
                wait(sp, mask_ready["L"], i * 1)
                settle(sp, i)
                sp.dma_start(mask_l8[:], t_mask_l[i].rearrange("(t p) k -> p t k", p=P)).then_inc(load["mask_l"], 16)

            load_batch(0, True)
            with sp.Fori(1, B - 1) as i:
                load_batch(i, True)
            load_batch(B - 1, False)
            with sp.Fori(0, B) as b:
                sp.wait_ge(results_ready, b + 1)
                settle(sp, b)
                sp.dma_start(t_out[b].rearrange("(t p) d -> p t d", p=P), x2[:, b, :, :]).then_inc(stored, 16)
            sp.wait_ge(stored, B * 16)

        @block.tensor
        def _(pe):
            def scores(job, b, h, t):
                g, j = h // HG, h % HG
                out = score_bank[t[1] % S_BANKS]
                if h == 0 and isinstance(b, int):
                    stage_taken(pe, "v", job, b, 0)
                    for n in range(4):
                        stage_taken(pe, "sel", job, b, n)
                if h == 0 and job == "A":
                    wait(pe, mask_ready["A"], b + 1)
                wait(pe, maxima_ready, times(t, NT, -NT * (S_BANKS - 1)))
                if job == "A":
                    pe.matmul(out[:], identity16[:], mask_a[:].rearrange("p t k -> p (t k)"), start=True, stop=False,
                              skip_group_check=True)
                for qt in range(NT):
                    last = pe.matmul(out[:, qt * S:(qt + 1) * S],
                                     q_stack[own(job, b)][32 * j:32 * j + 32, g, qt * P:(qt + 1) * P],
                                     k_stack[own(job, b)][32 * j:32 * j + 32, g, :], start=job != "A", stop=True,
                                     skip_group_check=True)
                last.then_inc(scores_ready, 1)

            def turn(h, t):
                out = turn_bank[h % T_BANKS]
                before = later(t, -T_BANKS)
                wait(pe, copied_dve if before[1] % HG in COPY_ON_DVE else copied_act,
                     copies(before, before[1] % HG in COPY_ON_DVE))
                wait(pe, exps_ready, times(t, NT, NT))
                for qt in range(NT):
                    for kt in range(NT):
                        last = pe.transpose(out[:, kt * S + qt * P:kt * S + (qt + 1) * P],
                                            probs[:, t[1] % N_PROBS, qt, kt * P:(kt + 1) * P], identity[:])
                last.then_inc(turned, 1)

            def weigh_values(place, g, t):
                n = g % 2
                for on_dve in (False, True):
                    wait(pe, copied_dve if on_dve else copied_act, copies(t, on_dve))
                wait(pe, heads_copied, group(t))
                for kt in range(NT):
                    for j in range(HG):
                        last = pe.matmul(head_bank[32 * j:32 * j + HD + 1, n * S:(n + 1) * S],
                                         values[place][:, kt, g * HG + j, :], probsT[:, n, j, kt, :],
                                         start=kt == 0, stop=kt == NT - 1, skip_group_check=True)
                last.then_inc(heads_ready, 1)

            def dense(use, t_fin):
                stage, job, b, part = use
                if stage in NO_PSUM:
                    return
                if stage == "fin":
                    wait(pe, heads_copied, group(t_fin) + 1)
                elif stage == "oT":
                    if isinstance(b, int) and b == 0:
                        pe.wait_ge(late_weights, 16)
                    stage_taken(pe, "fin", job, b, 1)
                elif stage == "oproj":
                    stage_taken(pe, "oT", job, b, 0)
                elif stage == "qk" and job == "L":
                    stage_taken(pe, "lT", job, b, 0)
                elif stage == "qk":
                    source = "xT" if job == "A" else "cT"
                    wait(pe, load[source], b * 16 + 16)
                elif stage == "sel":
                    wait(pe, split_done[job], b * 2 + 2)
                elif stage == "v" and job == "L":
                    stage_taken(pe, "lT", job, b, 0)
                elif stage == "lT":
                    normalised(pe, "K", b)
                    normalised(pe, "Q", b)
                elif stage == "ffT":
                    normalised(pe, "C", b)
                elif stage == "ff1":
                    stage_taken(pe, "ffT", job, b, 0)
                elif stage == "ff2":
                    stage_taken(pe, "ff1", job, b, 0)
                    stage_taken(pe, "ff1", job, b, 1)
                out, filled = stage_free(pe, *use)
                if stage == "fin":
                    for qt in range(NT):
                        for n in range(2):
                            at = (2 * qt + n) * P
                            last = pe.transpose(out[:, at:at + P], headsT[:, 2 * part + n, qt * P:(qt + 1) * P],
                                                identity[:])
                elif stage == "oT":
                    for qt in range(NT):
                        last = pe.transpose(out[:, qt * P:(qt + 1) * P], attended[job][:, qt, :], identity[:])
                elif stage == "oproj":
                    for qt in range(NT):
                        last = pe.matmul(out[:, qt * D:(qt + 1) * D], attendedT[:, qt * P:(qt + 1) * P],
                                         weight(job + "o"), start=True, stop=True)
                elif stage == "qk":
                    q_in = lT[:, 0, :] if job == "L" else xT[:]
                    k_in = {"A": xT[:], "C": cT[:], "L": lT[:, 1, :]}[job]
                    pe.matmul(out[:, 0:S], weight(job + "q"), q_in, start=True, stop=True)
                    last = pe.matmul(out[:, S:2 * S], weight(job + "k"), k_in, start=True, stop=True)
                elif stage == "sel":
                    side = part // 2
                    for n in range(2):
                        g = part % 2 * 2 + n
                        pe.matmul(out[:, n * S:(n + 1) * S], select[:, 2 * side, g, :], qk_high[:, side, :],
                                  start=True, stop=False)
                        last = pe.matmul(out[:, n * S:(n + 1) * S], select[:, 2 * side + 1, g, :],
                                         qk_low[:, side, :], start=False, stop=True)
                elif stage == "v":
                    source = {"A": xT[:], "C": cT[:], "L": lT[:, 1, :]}[job]
                    for kt in range(NT):
                        last = pe.matmul(out[:, kt * D:(kt + 1) * D], source[:, kt * P:(kt + 1) * P],
                                         weight(job + "v"), start=True, stop=True)
                elif stage == "lT":
                    for n, k in enumerate("QK"):
                        for qt in range(NT):
                            last = pe.transpose(out[:, n * S + qt * P:n * S + (qt + 1) * P], normed[k][:, qt, :],
                                                identity[:])
                elif stage == "ffT":
                    for qt in range(NT):
                        last = pe.transpose(out[:, qt * P:(qt + 1) * P], normed["C"][:, qt, :], identity[:])
                elif stage == "ff1":
                    last = hidden(out, "w1", part)
                elif stage == "ff2":
                    last = from_hidden(out, "w2", 0)
                last.then_inc(filled, 1)

            def hidden(out, w, part):
                for n in range(2):
                    at = W_FF[w] + (2 * part + n) * P
                    last = pe.matmul(out[:, n * S:(n + 1) * S], weights[:, at:at + P], ffT[:], start=True, stop=True)
                return last

            def from_hidden(out, w, buffer):
                for qt in range(NT):
                    for c in range(F // P):
                        at = W_FF[w] + c * D
                        last = pe.matmul(out[:, qt * D:(qt + 1) * D], hiddenT[:, buffer, c, qt * P:(qt + 1) * P],
                                         weights[:, at:at + D], start=c == 0, stop=c == F // P - 1)
                return last

            def warm(job, b, t0):
                for h in range(LEAD_S):
                    scores(job, b, h, later(t0, h))

            def step(h, kind, i, job, b, t0, prev, nxt):
                far = ahead(h, LEAD_S, job, b, t0, nxt)
                if far:
                    scores(*far)
                for use in stages(kind, i, h):
                    dense(use, last_head(use, t0, prev))
                if job:
                    turn(h, later(t0, h))
                if h == 1 and prev:
                    weigh_values(own(prev[0], prev[1]), NG - 1, later(prev[2], H - 1))
                elif h % HG == 1 and h > 1 and job:
                    g = h // HG - 1
                    weigh_values(own(job, b), g, later(t0, g * HG + HG - 1))

            def feed_forward(b, part):
                if part == 0:
                    pe.wait_ge(ln_steps["N"], (b + 1) * LN_STEPS["N"])
                    wait(pe, rows_copied, b)
                    for qt in range(NT):
                        last = pe.transpose(score_bank[0][:, qt * P:(qt + 1) * P], normed["A"][:, qt, :], identity[:])
                    last.then_inc(rows_turned, 1)
                elif part == 1:
                    pe.wait_ge(rows_copied, b + 1)
                    for n in range(2):
                        wait(pe, gelus_ready, b * 2 + (n - 1))
                        hidden(turn_bank[n], "fc1", n).then_inc(hidden_ready, 1)
                else:
                    pe.wait_ge(gelus_ready, b * 2 + 2)
                    wait(pe, results_ready, b)
                    from_hidden(score_bank[1], "fc2", b % 2).then_inc(out_ready, 1)

            def tick(k):
                for part in range(3):
                    if 0 <= k - part < B:
                        feed_forward(k - part, part)

            pe.wait_ge(constants, 5 * 16)
            pe.wait_ge(const_steps, 5)
            pe.wait_ge(pads_ready, 3)
            for stage, part in PREPARE:
                dense((stage, "A", 0, part), None)
            run_jobs(pe, warm, step, tick)

        @block.vector
        def _(dve):
            def maximum(job, b, h, t):
                source = score_bank[t[1] % S_BANKS]
                least = neg_max_a if job == "A" else neg_max_cl
                if job in "AC" and isinstance(b, int) and b == 0 and h % HG == 0:
                    dve.wait_ge(bias_in[job][h // HG], HG * 16)
                if job == "L" and h == 0:
                    wait(dve, mask_ready["L"], b + 1)
                wait(dve, scores_ready, times(t, 1, 1))
                wait(dve, exps_ready, times(t, NT, NT - N_SCORES * NT))
                settle(dve, b)
                for qt in range(NT):
                    dve.tensor_tensor_reduce(
                        out=neg_scores[:, t[1] % N_SCORES, qt, :], in0=source[:, qt * S:(qt + 1) * S],
                        in1=masks[own(job, b)][:, qt, :] if job == "L" else bias[job][:, h, qt, :], scale=-1.0, scalar=3.0e38,
                        op0=ALU.add, op1=ALU.min, accum_out=least[:, qt, h:h + 1]).then_inc(maxima_ready, 1)

            def copy_turned(h, t):
                n = (h // HG) % 2
                wait(dve, turned, times(t, 1, 1))
                wait(dve, heads_ready, group(t) - 1)
                dve.tensor_copy(probsT[:, n, h % HG, :, :].rearrange("p a b -> p (a b)"), turn_bank[h % T_BANKS][:])\
                    .then_inc(copied_dve, 1)

            def layer_norm(k, b, source, first=0):
                done, n = ln_steps[k], b * LN_STEPS[k] + first
                for qt in range(NT):
                    dve.bn_stats(out=stats[k][:, qt, :], in_=source(qt)).then_inc(done, 1)
                for qt in range(NT):
                    dve.wait_ge(done, n + 1 + qt)
                    settle(dve, b)
                    dve.bn_aggr(out=mean_var[k][:, qt, :], in_=stats[k][:, qt, :]).then_inc(done, 1)
                dve.wait_ge(done, n + 2 * NT)
                dve.tensor_scalar(mean_var[k][:, :, 1], mean_var[k][:, :, 1], EPS, None, ALU.add).then_inc(done, 1)
                to = normed["A"] if k == "N" else normed[k]
                for qt in range(NT):
                    dve.scalar_tensor_tensor(out=to[:, qt, :], in0=source(qt), scalar=mean_var[k][:, qt, 0:1],
                                             in1=vec(f"ln_{k}_g"), op0=ALU.subtract, op1=ALU.mult).then_inc(done, 1)

            def dense(use, t_fin):
                stage, job, b, part = use
                if stage == "fin":
                    source, read = stage_full(dve, *use)
                    rows = source[:].rearrange("p (t j c) -> p t j c", t=NT, j=H // 2)
                    steps = fins_before(t_fin) * 2
                    if job == "A":
                        dve.scalar_tensor_tensor(out=sums[:], in0=neg_max_a[:, :, part * H // 2:(part + 1) * H // 2],
                                                 scalar=-MASKED / 2, in1=rows[:, :, :, HD], op0=ALU.is_lt,
                                                 op1=ALU.mult).then_inc(fin_steps, 1)
                    else:
                        dve.tensor_copy(sums[:], rows[:, :, :, HD]).then_inc(fin_steps, 1)
                    dve.wait_ge(fin_steps, steps + 1)
                    dve.reciprocal(inverse[:], sums[:]).then_inc(fin_steps, 1)
                    dve.wait_ge(fin_steps, steps + 2)
                    to = attended[job][:, :, part * D // 2:(part + 1) * D // 2]\
                        .rearrange("p t (j c) -> p t j c", j=H // 2)
                    dve.tensor_tensor(to, rows[:, :, :, 0:HD], inverse[:].unsqueeze(3).broadcast_to([P, NT, H // 2, HD]),
                                      op=ALU.mult).then_inc(read, 1)
                elif stage == "oproj":
                    source, read = stage_full(dve, *use)
                    rows = source[:, 0:NT * D].rearrange("p (t d) -> p t d", t=NT)
                    if job == "L":
                        wait(dve, res_ready["L"], b + 1)
                        dve.tensor_tensor(x2[:, b, :, :], rows, residual["L"][:], op=ALU.add).then_inc(read, 1)
                    else:
                        if job == "A":
                            wait(dve, res_ready["A"], b + 1)
                        else:
                            normalised(dve, "A", b, 1)
                        dve.tensor_tensor(summed[:], rows, residual[job][:], op=ALU.add).then_inc(read, 1)
                        stage_taken(dve, *use)
                        layer_norm(job, b, lambda qt: summed[:, qt, :])
                elif stage == "split":
                    stage_taken(dve, "qk", job, b, 0)
                    dve.tensor_copy(qk_high[:], qk_plain[:]).then_inc(split_done[job], 1)
                    dve.wait_ge(split_done[job], b * 2 + 1)
                    dve.tensor_tensor(qk_low[:], qk_plain[:], qk_high[:].bitcast(f32), op=ALU.subtract)\
                        .then_inc(split_done[job], 1)
                elif stage == "sel" and part % 2 == 1:
                    source, read = stage_full(dve, *use)
                    to = (q_stack if part // 2 == 0 else k_stack)[own(job, b)]
                    dve.tensor_copy(to[:, 2:4, :].rearrange("p g s -> p (g s)"), source[:]).then_inc(read, 1)
                elif stage == "v" and job != "L":
                    source, read = stage_full(dve, *use)
                    dve.tensor_tensor(values[own(job, b)][:, :, :, 0:HD],
                                      source[:, 0:NT * D].rearrange("p (t h c) -> p t h c", t=NT, h=H),
                                      vec2(job + "v_b").rearrange("p t (h c) -> p t h c", h=H), op=ALU.add)\
                        .then_inc(read, 1)
                elif stage == "ff2":
                    source, read = stage_full(dve, *use)
                    rows = source[:, 0:NT * D].rearrange("p (t d) -> p t d", t=NT)
                    dve.tensor_tensor(ff_out[:], rows, vec2("ff_b2"), op=ALU.add).then_inc(read, 1)
                    stage_taken(dve, *use)
                    normalised(dve, "C", b)
                    dve.scalar_tensor_tensor(out=summed[:], in0=ff_out[:], scalar=0.0, in1=normed["C"][:],
                                             op0=ALU.max, op1=ALU.add).then_inc(ln_steps["F"], 1)
                    dve.wait_ge(ln_steps["F"], b * LN_STEPS["F"] + 1)
                    wait(dve, res_ready["L"], b * 1)
                    layer_norm("F", b, lambda qt: summed[:, qt, :], 1)
                elif stage == "lnQ":
                    normalised(dve, "F", b)
                    layer_norm("Q", b, lambda qt: normed["F"][:, qt, :])
                elif stage == "lnK":
                    dve.wait_ge(load["c"], b * 16 + 16)
                    layer_norm("K", b, lambda qt: c_tok[:, qt, :])

            def warm(job, b, t0):
                for h in range(LEAD_M):
                    maximum(job, b, h, later(t0, h))

            def step(h, kind, i, job, b, t0, prev, nxt):
                far = ahead(h, LEAD_M, job, b, t0, nxt)
                if far:
                    maximum(*far)
                if job and h % HG in COPY_ON_DVE and kind not in CROWDED:
                    copy_turned(h, later(t0, h))
                for use in stages(kind, i, h):
                    dense(use, last_head(use, t0, prev))
                if job and h % HG in COPY_ON_DVE and kind in CROWDED:
                    copy_turned(h, later(t0, h))

            def norm_rows(b):
                stage_taken(dve, "oproj", "L", b, 0)
                wait(dve, rows_turned, b)
                layer_norm("N", b, lambda qt: x2[:, b, qt, :])
                dve.wait_ge(ln_done["N"], b * LN_PARTS["N"] + 1)
                for qt in range(NT):
                    dve.wait_ge(ln_steps["N"], b * LN_STEPS["N"] + (2 * NT + 2 + qt))
                    dve.scalar_tensor_tensor(out=normed["A"][:, qt, :], in0=normed["A"][:, qt, :],
                                             scalar=rstd["N"][:, qt:qt + 1], in1=vec("ln_N_b"), op0=ALU.mult,
                                             op1=ALU.add).then_inc(ln_steps["N"], 1)

            def add_result(b):
                dve.wait_ge(ln_done["N"], b * LN_PARTS["N"] + 2)
                dve.wait_ge(out_ready, b + 1)
                dve.tensor_tensor(x2[:, b, :, :], score_bank[1][:, 0:NT * D].rearrange("p (t d) -> p t d", t=NT),
                                  x2[:, b, :, :], op=ALU.add).then_inc(results_ready, 1)

            def tick(k):
                if k == 0:
                    norm_rows(0)
                if k + 1 < B:
                    norm_rows(k + 1)
                if 0 <= k - 2 < B:
                    add_result(k - 2)

            dve.wait_ge(constants, 5 * 16)
            dve.tensor_copy(select[:].rearrange("p a g c -> p (a g c)"),
                            probsT[:, 0, :, :, :].rearrange("p a b c -> p (a b c)")).then_inc(const_steps, 1)
            dve.tensor_copy(identity16[:], identity[:]).then_inc(const_steps, 1)
            dve.memset(head_bank[:], 0.0).then_inc(const_steps, 1)
            for job in "AC":
                at = COLUMN[job + "q"]
                dve.tensor_scalar(columns[:, at:at + 1], columns[:, at:at + 1], SCALE[job], None, ALU.mult)\
                    .then_inc(const_steps, 1)
            for stage, part in PREPARE:
                dense((stage, "A", 0, part), None)
            run_jobs(dve, warm, step, tick)

        @block.scalar
        def _(act):
            def exponentials(h, t, job):
                least = neg_max_a if job == "A" else neg_max_cl
                wait(act, turned, times(t, 1, 1 - N_PROBS))
                for qt in range(NT):
                    wait(act, maxima_ready, times(t, NT, qt + 1))
                    act.activation(probs[:, t[1] % N_PROBS, qt, :], neg_scores[:, t[1] % N_SCORES, qt, :], ACT.Exp,
                                   bias=least[:, qt, h:h + 1], scale=-1.0).then_inc(exps_ready, 1)

            def copy_turned(h, t):
                n = (h // HG) % 2
                wait(act, turned, times(t, 1, 1))
                wait(act, heads_ready, group(t) - 1)
                act.activation(probsT[:, n, h % HG, :, :].rearrange("p a b -> p (a b)"), turn_bank[h % T_BANKS][:],
                               ACT.Copy).then_inc(copied_act, 1)

            def copy_heads(t, g):
                n = g % 2
                wait(act, heads_ready, group(t) + 1)
                act.activation(headsT[:, g, :], head_bank[:, n * S:(n + 1) * S], ACT.Copy).then_inc(heads_copied, 1)

            def dense(use):
                stage, job, b, part = use
                if stage == "qk":
                    source, read = stage_full(act, *use)
                    if job == "L":
                        act.activation(qk_plain[:, 0, :], source[:, 0:S], ACT.Copy, scale=SCALE[job])
                        act.activation(qk_plain[:, 1, :], source[:, S:2 * S], ACT.Copy).then_inc(read, 1)
                    else:
                        at = COLUMN[job + "q"]
                        act.activation(qk_plain[:, 0, :], source[:, 0:S], ACT.Identity, bias=columns[:, at:at + 1],
                                       scale=SCALE[job])
                        act.activation(qk_plain[:, 1, :], source[:, S:2 * S], ACT.Identity,
                                       bias=columns[:, at + 1:at + 2]).then_inc(read, 1)
                elif stage == "sel" and part % 2 == 0:
                    source, read = stage_full(act, *use)
                    to = (q_stack if part // 2 == 0 else k_stack)[own(job, b)]
                    act.activation(to[:, 0:2, :].rearrange("p g s -> p (g s)"), source[:], ACT.Copy).then_inc(read, 1)
                elif stage == "v" and job == "L":
                    source, read = stage_full(act, *use)
                    act.activation(values[own(job, b)][:, :, :, 0:HD],
                                   source[:, 0:NT * D].rearrange("p (t h c) -> p t h c", t=NT, h=H), ACT.Copy)\
                        .then_inc(read, 1)
                elif stage in ("oT", "ffT"):
                    source, read = stage_full(act, *use)
                    act.activation((attendedT if stage == "oT" else ffT)[:], source[:, 0:S], ACT.Copy).then_inc(read, 1)
                elif stage == "lT":
                    source, read = stage_full(act, *use)
                    act.activation(lT[:].rearrange("p a s -> p (a s)"), source[:], ACT.Copy).then_inc(read, 1)
                elif stage == "ff1":
                    source, read = stage_full(act, *use)
                    hidden(source, part, ACT.Relu, "b1", 0).then_inc(read, 1)

            def hidden(source, part, func, bias_name, buffer):
                for n in range(2):
                    c = 2 * part + n
                    at = COLUMN[bias_name] + c
                    last = act.activation(hiddenT[:, buffer, c, :], source[:, n * S:(n + 1) * S], func,
                                          bias=columns[:, at:at + 1])
                return last

            def warm(job, b, t0):
                for h in range(LEAD_E):
                    exponentials(h, later(t0, h), job)

            def step(h, kind, i, job, b, t0, prev, nxt):
                far = ahead(h, LEAD_E, job, b, t0, nxt)
                if far:
                    exponentials(far[2], far[3], far[0])
                if kind in CROWDED:
                    for use in stages(kind, i, h):
                        dense(use)
                if job and h % HG not in COPY_ON_DVE:
                    copy_turned(h, later(t0, h))
                if h == 2 and prev:
                    copy_heads(later(prev[2], H - 1), NG - 1)
                elif h % HG == 2 and h > 2 and job:
                    copy_heads(later(t0, (h // HG - 1) * HG), h // HG - 1)
                if kind not in CROWDED:
                    for use in stages(kind, i, h):
                        dense(use)

            def copy_rows(b):
                act.wait_ge(rows_turned, b + 1)
                wait(act, hidden_ready, b * 2)
                act.activation(ffT[:], score_bank[0][:, 0:S], ACT.Copy).then_inc(rows_copied, 1)

            def gelus(b):
                wait(act, out_ready, b - 1)
                for n in range(2):
                    act.wait_ge(hidden_ready, b * 2 + (n + 1))
                    hidden(turn_bank[n], n, ACT.Gelu, "fc1_b", b % 2).then_inc(gelus_ready, 1)

            def tick(k):
                if k < B:
                    copy_rows(k)
                if 0 <= k - 1 < B:
                    gelus(k - 1)

            act.wait_ge(constants, 5 * 16)
            act.wait_ge(const_steps, 5)
            for stage, part in PREPARE:
                dense((stage, "A", 0, part))
            run_jobs(act, warm, step, tick)

        @block.gpsimd
        def _(pool):
            def normalise(k, b):
                to, n = normed[k], b * LN_PARTS[k]
                wait(pool, ln_steps[k], b * LN_STEPS[k] + (LN_STEPS[k] - NT))
                pool.tensor_tensor(rstd[k][:], mean_var[k][:, :, 1], minus_half[:], op=ALU.pow).then_inc(ln_done[k], 1)
                wait(pool, ln_done[k], n + 1)
                wait(pool, ln_steps[k], b * LN_STEPS[k] + LN_STEPS[k])
                pool.tensor_tensor(to[:], to[:], rstd[k][:].unsqueeze(2).broadcast_to([P, NT, D]), op=ALU.mult)\
                    .then_inc(ln_done[k], 1)
                wait(pool, ln_done[k], n + 2)
                pool.tensor_tensor(to[:], to[:], vec2(f"ln_{k}_b"), op=ALU.add).then_inc(ln_done[k], 1)

            def dense(use, t_before):
                stage, job, b, part = use
                if stage == "maskA":
                    wait(pool, load["mask_a"], b * 16 + 16)
                    if t_before:
                        wait(pool, scores_ready, times(t_before))
                    settle(pool, b)
                    pool.tensor_scalar(mask_a[:], mask_a8[:], MASKED, None, ALU.mult).then_inc(mask_ready["A"], 1)
                elif stage == "maskL":
                    wait(pool, load["mask_l"], b * 16 + 16)
                    if t_before:
                        wait(pool, maxima_ready, times(t_before, NT))
                    settle(pool, b)
                    pool.tensor_scalar(masks[own("L", b)][:], mask_l8[:], MASKED, None, ALU.mult).then_inc(mask_ready["L"], 1)
                elif stage == "resA":
                    wait(pool, load["x"], b * 16 + 16)
                    wait(pool, ln_steps["A"], b * LN_STEPS["A"] - 3 * NT)
                    pool.tensor_tensor(residual["A"][:], x_tok[:], vec2("Ao_b"), op=ALU.add).then_inc(res_ready["A"], 1)
                elif stage == "oproj" and job in "AC":
                    normalise(job, b)
                    if job == "A":
                        normalised(pool, "A", b)
                        pool.tensor_tensor(residual["C"][:], normed["A"][:], vec2("Co_b"), op=ALU.add)\
                            .then_inc(ln_done["A"], 1)
                elif stage == "ff2":
                    normalise("F", b)
                elif stage in ("lnQ", "lnK"):
                    normalise(job, b)
                elif stage == "resL":
                    if not isinstance(b, int) or b > 0:
                        stage_taken(pool, "oproj", "L", b - 1, 0)
                    normalised(pool, "F", b)
                    pool.tensor_tensor(residual["L"][:], normed["F"][:], vec2("Lo_b"), op=ALU.add)\
                        .then_inc(res_ready["L"], 1)

            def step(h, kind, i, job, b, t0, prev, nxt):
                for use in stages(kind, i, h):
                    dense(use, later(prev[2], H) if prev else None)

            pool.memset(minus_half[:], -0.5).then_inc(halves_ready, 1)
            pool.wait_ge(halves_ready, 1)
            def rows(b):
                pool.wait_ge(ln_steps["N"], b * LN_STEPS["N"] + (2 * NT + 1))
                pool.tensor_tensor(rstd["N"][:], mean_var["N"][:, :, 1], minus_half[:], op=ALU.pow)\
                    .then_inc(ln_done["N"], 1)
                pool.wait_ge(ln_steps["N"], b * LN_STEPS["N"] + (3 * NT + 1))
                pool.tensor_tensor(x2[:, b, :, :], x2[:, b, :, :], vec2("fc2_b"), op=ALU.add).then_inc(ln_done["N"], 1)

            def tick(k):
                if k == 0:
                    rows(0)
                if k + 1 < B:
                    rows(k + 1)

            for job in "ACL":
                pool.memset(values[job][:, :, :, HD:HD + 1], 1.0).then_inc(pads_ready, 1)
            dense(("maskA", "A", 0, 0), None)
            pool.wait_ge(constants, 5 * 16)
            dense(("resA", "A", 0, 0), None)
            run_jobs(pool, lambda *_: None, step, tick)


def selections():
    import numpy as np
    m = np.zeros((P, PARTS, NG, P), np.float32)
    for g in range(NG):
        for j in range(HG):
            for part in range(PARTS):
                for d in range(HD):
                    row, col = (g * HG + j) * HD + d, 32 * j + HD * part + d
                    m[row, part // 2, g, col] = 1.0
                    m[row, 2 + part % 2, g, col] = 1.0
    return m.reshape(P, PARTS * NG * P)


def kernel(**inputs):
    import numpy as np
    import concourse.bacc as bacc
    from concourse.bass_utils import run_bass_kernel_spmd

    a = {k: np.asarray(v) for k, v in inputs.items()}
    l0, l1 = "L0_xattn_", "L1_xattn_"
    kv = a[l1 + "kv_w"]
    square = [a[l0 + "sa_wq"], a[l0 + "sa_wk"], a[l0 + "sa_wv"], a[l0 + "ca_wq"], a[l0 + "ca_wk"], a[l0 + "ca_wv"],
              a[l0 + "sa_wo"], a[l0 + "ca_wo"], a[l1 + "q_w"], kv[:, :D], kv[:, D:], a[l1 + "proj_w"]]

    def by_rows(w):
        return w.reshape(F // P, P, D).transpose(1, 0, 2).reshape(P, F)

    weights = np.concatenate(square + [a[l0 + "ff_w1"], by_rows(a[l0 + "ff_w2"]), a[l1 + "fc1_w"],
                                       by_rows(a[l1 + "fc2_w"])], axis=1)
    columns = np.concatenate([a[l0 + n].reshape(-1, P) for n in ("sa_bq", "sa_bk", "ca_bq", "ca_bk", "ff_b1")]
                             + [a[l1 + "fc1_b"].reshape(-1, P)], axis=0).T
    names = {"Av_b": l0 + "sa_bv", "Cv_b": l0 + "ca_bv", "Ao_b": l0 + "sa_bo", "Co_b": l0 + "ca_bo",
             "Lo_b": l1 + "proj_b", "ln_A_g": l0 + "sa_g", "ln_A_b": l0 + "sa_b", "ln_C_g": l0 + "ca_g",
             "ln_C_b": l0 + "ca_b", "ln_F_g": l0 + "ff_g", "ln_F_b": l0 + "ff_b", "ln_Q_g": l1 + "qn_w",
             "ln_Q_b": l1 + "qn_b", "ln_K_g": l1 + "cn_w", "ln_K_b": l1 + "cn_b", "ln_N_g": l1 + "n2_w",
             "ln_N_b": l1 + "n2_b", "ff_b2": l0 + "ff_b2", "fc2_b": l1 + "fc2_b"}
    arrays = {
        "x": a["x"], "x_turned": a["x"].transpose(0, 2, 1),
        "ctx": a["ctx_1024"], "ctx_turned": a["ctx_1024"].transpose(0, 2, 1),
        "mask_self": a["mask_BxSxS2_bk1"], "mask_cross": a["mask_BxSxS2_bk0"],
        "bias_self": a["fside_1x16xSxS2_0"][0], "bias_cross": a[l0 + "attn_2d_bias"][0],
        "weights": weights, "columns": columns, "vectors": np.stack([a[names[n]] for n in VECTORS]),
        "selections": selections(), "identity": np.eye(P, dtype=np.float32),
    }
    nc = bacc.Bacc("TRN2", target_bir_lowering=False, num_devices=1)
    args = []
    for name in arrays:
        arrays[name] = np.ascontiguousarray(arrays[name])
        args.append(nc.dram_tensor("in_" + name, arrays[name].shape, mybir.dt.from_np(arrays[name].dtype),
                                   kind="ExternalInput").ap())
    args.append(nc.dram_tensor("out", (B, S, D), mybir.dt.float32, kind="ExternalOutput").ap())
    two_layers(nc, *args)
    r = run_bass_kernel_spmd(nc, [{"in_" + n: v for n, v in arrays.items()}], core_ids=[0])
    return r.results[0]["out"]
```

```python
import concourse.bass as bass
from concourse import mybir
from contextlib import ExitStack


B, S, D, H, F = 8, 256, 128, 16, 512
P = 128
HD = D // H
NT = S // P
HG = 4
NG = H // HG
PARTS = 4
PARTS_OF = [slice(0, 4, 3), slice(0, 3, 2), slice(1, 4, 2), slice(1, 3)]
EPS = 1e-5
MASKED = -2.0 ** 100
SCALE = {"A": float(D) ** -0.5, "C": float(D) ** -0.5, "L": float(HD) ** -0.5}

WEIGHTS = ["Aq", "Ak", "Av", "Cq", "Ck", "Cv", "Ao", "Co", "Lq", "Lk", "Lv", "Lo"]
W_FF = {"w1": 12 * D, "w2": 12 * D + F, "fc1": 12 * D + 2 * F, "fc2": 12 * D + 3 * F}
W_COLS = 12 * D + 4 * F
COLUMN = {"Aq": 0, "Ak": 1, "Cq": 2, "Ck": 3, "b1": 4, "fc1_b": 8}
N_COLUMN = 12
VECTORS = ["Av_b", "Cv_b", "Ao_b", "Co_b", "Lo_b", "ln_A_g", "ln_A_b", "ln_C_g", "ln_C_b", "ln_F_g", "ln_F_b",
           "ln_Q_g", "ln_Q_b", "ln_K_g", "ln_K_b", "ln_N_g", "ln_N_b", "ff_b2", "fc2_b"]

LEAD_S, LEAD_M, LEAD_E = 4, 3, 2
S_BANKS, T_BANKS, STAGE_BANKS = 4, 2, 1
N_PROBS = 3
COPY_ON_DVE, COPY_PERIOD = (2, 6), 8

STEPS = {
    "first": {0: [("qk", "C", 1, 0)], 1: [("split", "C", 1, 0)], 4: [("v", "C", 1, 0)], 13: [("fin", "A", 1, 0)]},
    "C": {0: [("qk", "A", 1, 0)], 2: [("v", "A", 1, 0)], 3: [("split", "A", 1, 0)], 4: [("fin", "A", 0, 1)],
          7: [("oT", "A", 0, 0)], 9: [("oproj", "A", 0, 0)], 12: [("fin", "C", 0, 0)],
          13: [("maskA", "A", 1, 0)]},
    "start": {0: [("qk", "C", 1, 0)], 2: [("split", "C", 1, 0), ("v", "C", 1, 0)],
              4: [("fin", "C", 0, 1), ("oT", "C", 0, 0), ("resA", "A", 1, 0)], 5: [("oproj", "C", 0, 0)],
              7: [("ffT", "F", 0, 0)], 8: [("ff1", "F", 0, 0), ("ff1", "F", 0, 1)],
              9: [("lnK", "K", 0, 0), ("ff2", "F", 0, 0)],
              12: [("fin", "A", 1, 0), ("resL", "L", 0, 0), ("lnQ", "Q", 0, 0), ("maskL", "L", 0, 0), ("lT", "L", 0, 0)],
              13: [("qk", "L", 0, 0)], 14: [("split", "L", 0, 0), ("v", "L", 0, 0)]},
    "L": {1: [("qk", "C", 1, 0)], 2: [("split", "C", 1, 0)], 4: [("v", "C", 1, 0)], 6: [("fin", "C", 0, 1)],
          7: [("oT", "C", 0, 0), ("resA", "A", 1, 0)], 9: [("oproj", "C", 0, 0)], 12: [("ffT", "F", 0, 0)],
          13: [("fin", "L", -1, 0)], 14: [("ff1", "F", 0, 0)], 15: [("ff1", "F", 0, 1)]},
    "A": {0: [("lnK", "K", 0, 0)], 1: [("ff2", "F", 0, 0)], 3: [("lnQ", "Q", 0, 0)], 4: [("fin", "L", -1, 1)],
          6: [("oT", "L", -1, 0)], 7: [("lT", "L", 0, 0)], 8: [("oproj", "L", -1, 0)], 9: [("qk", "L", 0, 0)],
          10: [("split", "L", 0, 0), ("v", "L", 0, 0), ("resL", "L", 0, 0)],
          12: [("fin", "A", 1, 0), ("maskL", "L", 0, 0)]},
    "end": {4: [("fin", "C", 0, 1), ("oT", "C", 0, 0)], 5: [("oproj", "C", 0, 0)], 7: [("ffT", "F", 0, 0)],
            8: [("maskL", "L", 0, 0), ("ff1", "F", 0, 0), ("ff1", "F", 0, 1)],
            9: [("lnK", "K", 0, 0), ("ff2", "F", 0, 0)], 10: [("lnQ", "Q", 0, 0)], 11: [("fin", "L", -1, 0)],
            12: [("lT", "L", 0, 0)], 13: [("qk", "L", 0, 0)], 14: [("split", "L", 0, 0), ("v", "L", 0, 0)]},
    "last": {4: [("fin", "L", -1, 1)], 6: [("oT", "L", -1, 0)], 8: [("oproj", "L", -1, 0)],
             10: [("resL", "L", 0, 0)], 12: [("fin", "L", 0, 0)]},
    "drain": {4: [("fin", "L", 0, 1)], 6: [("oT", "L", 0, 0)], 8: [("oproj", "L", 0, 0)]},
}
TICK_AT = {3: 0, 4: 1, 5: 2, 6: 3, 7: 4, 8: 5, 11: 6, 13: 7, 14: 8, 15: 9}
NO_PSUM = ("maskA", "maskL", "resA", "resL", "lnK", "lnQ", "split")
PREPARE = ["qk", "split", "v"]


def stages(kind, i, h):
    known = isinstance(i, int)
    return [(s, j, i + d, p) for s, j, d, p in STEPS[kind].get(h, []) if not known or 0 <= i + d < B]


def number_stage_banks():
    found, before = {}, [0] * STAGE_BANKS

    def segment(uses):
        for n, use in enumerate(uses):
            found[use] = (n % STAGE_BANKS, before[n % STAGE_BANKS])
            before[n % STAGE_BANKS] += 1

    def of(kind, i):
        return [u for h in range(H) for u in stages(kind, i, h) if u[0] not in NO_PSUM]

    segment([(s, "A", 0, 0) for s in PREPARE if s not in NO_PSUM] + of("first", -1) + of("C", 0) + of("start", 0))
    for i in range(1, B - 1):
        segment(of("C", i) + of("L", i) + of("A", i))
    segment(of("C", B - 1) + of("end", B - 1) + of("last", B - 1) + of("drain", B - 1))
    return found


USES = number_stage_banks()


def two_layers(nc: bass.Bass, t_x, t_xT, t_c, t_cT, t_mask_a, t_mask_l, t_bias_a, t_bias_c, t_weights, t_columns,
               t_vectors, t_identity, t_out):
    f32, f32r, bf16, u8 = mybir.dt.float32, mybir.dt.float32r, mybir.dt.bfloat16, mybir.dt.uint8
    ALU, ACT = mybir.AluOpType, mybir.ActivationFunctionType

    with ExitStack() as ctx:
        def sb(name, shape, dt=f32):
            return ctx.enter_context(nc.sbuf_tensor(name, shape, dt))

        def bank(name):
            return ctx.enter_context(nc.psum_tensor(name, [P, 512], f32))

        def sem(name):
            return ctx.enter_context(nc.semaphore(name))

        bias = {"A": sb("bias_a", [P, H, NT, S]), "C": sb("bias_c", [P, H, NT, S])}
        stacks = {j: sb(f"stacks_{j}", [P, 2, NG, S], f32r) for j in "ACL"}
        values = {j: sb(f"values_{j}", [P, NT, H, HD + 1]) for j in "ACL"}
        neg_max_a = sb("neg_max_a", [P, NT, H])
        neg_max_cl = sb("neg_max_cl", [P, NT, H])
        probs = sb("probs", [P, N_PROBS, NT, S])
        probsT = sb("probsT", [P, 2, HG, NT, S])
        headsT = sb("headsT", [P, NG, S])
        sums = sb("sums", [P, NT, H // 2])
        inverse = sb("inverse", [P, NT, H // 2])
        attended = {j: sb(f"attended_{j}", [P, NT, D]) for j in "ACL"}
        attendedT = sb("attendedT", [P, S])
        qk_plain = sb("qk_plain", [P, 2, S])
        qk_parts = {j: sb(f"qk_parts_{j}", [P, 4, S], f32r) for j in "ACL"}
        weights = sb("weights", [P, W_COLS])
        columns = sb("columns", [P, N_COLUMN])
        vectors = sb("vectors", [P, len(VECTORS), D])
        identity = sb("identity", [P, P])
        identity16 = sb("identity16", [P, P], bf16)
        xT, cT = sb("xT", [P, S]), sb("cT", [P, S])
        x_tok, c_tok = sb("x_tok", [P, NT, D]), sb("c_tok", [P, NT, D])
        mask_a8, mask_l8 = sb("mask_a8", [P, NT, S], u8), sb("mask_l8", [P, NT, S], u8)
        mask_a, mask_l = sb("mask_a", [P, NT, S], bf16), sb("mask_l", [P, NT, S], bf16)
        masks = {"A": mask_a, "L": mask_l}
        residual = {j: sb(f"residual_{j}", [P, NT, D]) for j in "ACL"}
        summed = sb("summed", [P, NT, D])
        ff_out = sb("ff_out", [P, NT, D])
        normed = {k: sb(f"normed_{k}", [P, NT, D]) for k in "ACFQK"}
        stats = {k: sb(f"stats_{k}", [P, NT, 6]) for k in "ACFQKN"}
        minus_half, warm_up = sb("minus_half", [P, NT]), sb("warm_up", [P, NT])
        mean_var = {k: sb(f"mean_var_{k}", [P, NT, 2]) for k in "ACFQKN"}
        rstd = {k: sb(f"rstd_{k}", [P, NT]) for k in "ACFQKN"}
        ffT = sb("ffT", [P, S])
        hiddenT = sb("hiddenT", [P, 2, F // P, S])
        lT = sb("lT", [P, 2, S])
        x2 = sb("x2", [P, B, NT, D])

        def vec(name):
            return vectors[:, VECTORS.index(name), :]

        def vec2(name):
            return vectors[:, VECTORS.index(name):VECTORS.index(name) + 1, :].broadcast_to([P, NT, D])

        def weight(name):
            n = WEIGHTS.index(name)
            return weights[:, n * D:(n + 1) * D]

        score_bank = [bank(f"score_bank{n}") for n in range(S_BANKS)]
        turn_bank = [bank(f"turn_bank{n}") for n in range(T_BANKS)]
        head_bank = bank("head_bank")
        stage_bank = [bank(f"stage_bank{n}") for n in range(STAGE_BANKS)]

        scores_ready = sem("scores_ready")
        maxima_ready = sem("maxima_ready")
        exps_ready = sem("exps_ready")
        turned = sem("turned")
        copied_act = sem("copied_act")
        copied_dve = sem("copied_dve")
        heads_ready = sem("heads_ready")
        heads_copied = sem("heads_copied")
        fin_steps = sem("fin_steps")
        stage_filled = [sem(f"stage_filled{n}") for n in range(STAGE_BANKS)]
        stage_read = [sem(f"stage_read{n}") for n in range(STAGE_BANKS)]
        split_done = {j: sem(f"split_done_{j}") for j in "ACL"}
        ln_steps = {k: sem(f"ln_steps_{k}") for k in "ACFQKN"}
        ln_done = {k: sem(f"ln_done_{k}") for k in "ACFQKN"}
        mask_ready = {j: sem(f"mask_ready_{j}") for j in "AL"}
        res_ready = {j: sem(f"res_ready_{j}") for j in "AL"}
        rows_turned = sem("rows_turned")
        rows_copied = sem("rows_copied")
        hidden_ready = sem("hidden_ready")
        gelus_ready = sem("gelus_ready")
        out_ready = sem("out_ready")
        results_ready = sem("results_ready")
        constants = sem("constants")
        weights_c = sem("weights_c")
        late_weights = sem("late_weights")
        const_steps = sem("const_steps")
        pads_ready = sem("pads_ready")
        halves_ready = sem("halves_ready")
        stacks_in = {j: [sem(f"stacks_in_{j}{g}") for g in range(NG)] for j in "ACL"}
        bias_in = {j: [sem(f"bias_in_{j}{g}") for g in range(NG)] for j in "AC"}
        load = {n: sem(f"load_{n}") for n in ("xT", "cT", "x", "c", "mask_a", "mask_l")}
        stored = sem("stored")

        STACK_DMAS = 16 * PARTS
        LN_STEPS = {k: 3 * NT + (2 if k == "F" else 1) for k in "ACFQK"} | {"N": 4 * NT + 1}
        LN_PARTS = {k: 4 if k == "A" else 3 for k in "ACFQK"} | {"N": 2}

        def wait(eng, semaphore, value):
            if not isinstance(value, int) or value > 0:
                eng.wait_ge(semaphore, value)

        def settle(eng, value):
            if not isinstance(value, int):
                eng.nop(nofuse=True)

        OFFSET = {(s, j, p): d for kind in "CLA" for u in STEPS[kind].values() for s, j, d, p in u}

        def normalised(eng, k, b, plus=0):
            wait(eng, ln_done[k], b * LN_PARTS[k] + (3 + plus))

        def use_of(stage, job, b, part):
            if isinstance(b, int):
                return USES[(stage, job, b, part)]
            b2 = 2 + OFFSET[(stage, job, part)]
            at, first = USES[(stage, job, b2, part)]
            _, second = USES[(stage, job, b2 + 1, part)]
            return at, b * (second - first) + (first - b2 * (second - first))

        def stage_taken(eng, stage, job, b, part):
            at, before = use_of(stage, job, b, part)
            wait(eng, stage_read[at], before + 1)

        def stage_full(eng, stage, job, b, part):
            at, before = use_of(stage, job, b, part)
            wait(eng, stage_filled[at], before + 1)
            return stage_bank[at], stage_read[at]

        def stage_free(eng, stage, job, b, part):
            at, before = use_of(stage, job, b, part)
            wait(eng, stage_read[at], before)
            return stage_bank[at], stage_filled[at]

        PER = 3 * H

        def times(t, per=1, plus=0):
            i, c = t
            return i * (PER * per) + (c * per + plus)

        def copies(t, on_dve):
            i, c = t
            mine = [h for h in range(COPY_PERIOD) if (h in COPY_ON_DVE) == on_dve]
            return i * (PER // COPY_PERIOD * len(mine)) \
                + (c // COPY_PERIOD * len(mine) + sum(h <= c % COPY_PERIOD for h in mine))

        def group(t):
            i, c = t
            return i * (PER // HG) + c // HG

        def fins_before(t):
            i, c = t
            return i * (PER // (H // 2)) + c // (H // 2)

        def later(t, n):
            return t[0], t[1] + n

        def run_jobs(eng, warm, step, tick):
            def slot(kind, i, job, b, t0, prev, nxt):
                for h in range(H):
                    step(h, kind, i, job, b, t0, prev, nxt)

            warm("A", 0, (0, 0))
            slot("first", -1, "A", 0, (0, 0), None, ("C", 0, (0, 16)))
            slot("C", 0, "C", 0, (0, H), ("A", 0, (0, 0)), ("A", 1, (0, 2 * H)))
            slot("start", 0, "A", 1, (0, 2 * H), ("C", 0, (0, H)), ("C", 1, (1, 0)))
            with eng.Fori(1, B - 1) as i:
                slot("C", i, "C", i, (i, 0), ("A", i, (i, -H)), ("L", i - 1, (i, H)))
                slot("L", i, "L", i - 1, (i, H), ("C", i, (i, 0)), ("A", i + 1, (i, 2 * H)))
                slot("A", i, "A", i + 1, (i, 2 * H), ("L", i - 1, (i, H)), ("C", i + 1, (i, 3 * H)))
            z = B - 1
            slot("C", z, "C", z, (z, 0), ("A", z, (z, -H)), ("L", z - 1, (z, H)))
            slot("end", z, "L", z - 1, (z, H), ("C", z, (z, 0)), None)
            warm("L", z, (z, 2 * H))
            slot("last", z, "L", z, (z, 2 * H), ("L", z - 1, (z, H)), None)
            for h in range(H):
                step(h, "drain", z, None, 0, None, ("L", z, (z, 2 * H)), None)
                if h in TICK_AT:
                    tick(TICK_AT[h])

        def ahead(h, lead, job, b, t0, nxt):
            if job is None:
                return None
            if h + lead < H:
                return job, b, h + lead, later(t0, h + lead)
            if nxt is None:
                return None
            return nxt[0], nxt[1], h + lead - H, later(nxt[2], h + lead - H)

        def own(job, b):
            return "A" if job == "L" and isinstance(b, int) and b == B - 1 else job

        def last_head(use, t0, prev):
            if use[0] != "fin":
                return None
            return later(t0, H // 2 - 1) if use[3] == 0 else later(prev[2], H - 1)

        block = ctx.enter_context(nc.Block())

        @block.sync
        def _(sp):
            def stack(job, b, t_free):
                wait(sp, split_done[job], b * 2 + 2)
                settle(sp, b)
                wait(sp, scores_ready, times(t_free))
                settle(sp, b)
                for g in range(NG):
                    rows = slice(g * HG * HD, (g + 1) * HG * HD)
                    for part, source in enumerate(PARTS_OF):
                        sp.dma_start(stacks[own(job, b)][part:P:PARTS, :, g, :].bitcast(f32),
                                     qk_parts[job][rows, source, :].bitcast(f32)).then_inc(stacks_in[job][g], 16)

            def load_batch(i, last=False):
                first = isinstance(i, int) and i == 0
                c0 = (0, H) if first else (i, 0)
                if not last:
                    wait(sp, mask_ready["A"], i + 1)
                    settle(sp, i)
                    sp.dma_start(mask_a8[:], t_mask_a[i + 1].rearrange("(t p) k -> p t k", p=P))\
                        .then_inc(load["mask_a"], 16)
                    wait(sp, res_ready["A"], i + 1)
                    settle(sp, i)
                    sp.dma_start(x_tok[:], t_x[i + 1].rearrange("(t p) d -> p t d", p=P)).then_inc(load["x"], 16)
                wait(sp, ln_steps["K"], i * LN_STEPS["K"])
                settle(sp, i)
                sp.dma_start(c_tok[:], t_c[i].rearrange("(t p) d -> p t d", p=P)).then_inc(load["c"], 16)
                wait(sp, mask_ready["L"], i * 1)
                settle(sp, i)
                sp.dma_start(mask_l8[:], t_mask_l[i].rearrange("(t p) k -> p t k", p=P)).then_inc(load["mask_l"], 16)
                if not last:
                    stack("A", i + 1, c0)
                    wait(sp, heads_ready, group(c0) + 1)
                    settle(sp, i)
                    sp.dma_start(cT[:], t_cT[i + 1]).then_inc(load["cT"], 16)
                    stack("C", i + 1, later(c0, H))
                    if not isinstance(i, int) or i + 2 < B:
                        load_xT(i + 2)
                stack("L", i, later(c0, 2 * H) if not last else c0)

            def load_xT(b):
                wait(sp, split_done["C"], b * 2)
                settle(sp, b)
                sp.dma_start(xT[:], t_xT[b]).then_inc(load["xT"], 16)

            def load_bias(job, g):
                source = {"A": t_bias_a, "C": t_bias_c}[job]
                heads = slice(g * HG, (g + 1) * HG)
                sp.dma_start(bias[job][:, heads, :, :].rearrange("p h t k -> p (h t) k"),
                             source[heads].rearrange("h (t p) k -> p (h t) k", p=P)).then_inc(bias_in[job][g], 16)

            def load_vectors(first, last, signal):
                sp.dma_start(vectors[:, first:last, :], t_vectors[first:last].rearrange("(a n) d -> a n d", a=1)
                             .broadcast_to([P, last - first, D])).then_inc(signal, 16)

            sp.dma_start(xT[:], t_xT[0]).then_inc(load["xT"], 16)
            sp.dma_start(weights[:, 0:3 * D], t_weights[:, 0:3 * D]).then_inc(constants, 16)
            sp.dma_start(columns[:], t_columns).then_inc(constants, 16)
            sp.dma_start(identity[:], t_identity).then_inc(constants, 16)
            load_vectors(0, 2, constants)
            sp.dma_start(mask_a8[:], t_mask_a[0].rearrange("(t p) k -> p t k", p=P)).then_inc(load["mask_a"], 16)
            load_bias("A", 0)
            sp.dma_start(cT[:], t_cT[0]).then_inc(load["cT"], 16)
            sp.dma_start(weights[:, 3 * D:6 * D], t_weights[:, 3 * D:6 * D]).then_inc(weights_c, 16)
            load_bias("A", 1)
            stack("A", 0, (0, 0))
            load_bias("A", 2)
            load_bias("A", 3)
            load_bias("C", 0)
            stack("C", 0, (0, 0))
            load_xT(1)
            sp.dma_start(x_tok[:], t_x[0].rearrange("(t p) d -> p t d", p=P)).then_inc(load["x"], 16)
            load_bias("C", 1)
            sp.dma_start(weights[:, 6 * D:], t_weights[:, 6 * D:]).then_inc(late_weights, 16)
            load_vectors(2, len(VECTORS), late_weights)
            for g in range(2, NG):
                load_bias("C", g)
            load_batch(0)
            with sp.Fori(1, B - 2) as i:
                load_batch(i)
            load_batch(B - 2)
            load_batch(B - 1, last=True)
            with sp.Fori(0, B) as b:
                sp.wait_ge(results_ready, b + 1)
                settle(sp, b)
                sp.dma_start(t_out[b].rearrange("(t p) d -> p t d", p=P), x2[:, b, :, :]).then_inc(stored, 16)
            sp.wait_ge(stored, B * 16)

        @block.tensor
        def _(pe):
            def scores(job, b, h, t):
                g, j = h // HG, h % HG
                out = score_bank[t[1] % S_BANKS]
                if h == 0 and isinstance(b, int):
                    stage_taken(pe, "v", job, b, 0)
                if j == 0:
                    wait(pe, stacks_in[job][g], b * STACK_DMAS + STACK_DMAS)
                if h == 0 and job == "A":
                    wait(pe, mask_ready["A"], b + 1)
                wait(pe, exps_ready, times(t, NT, -NT * (S_BANKS - 1)))
                if job == "A":
                    pe.matmul(out[:], identity16[:], mask_a[:].rearrange("p t k -> p (t k)"), start=True, stop=False,
                              skip_group_check=True)
                for qt in range(NT):
                    last = pe.matmul(out[:, qt * S:(qt + 1) * S],
                                     stacks[own(job, b)][32 * j:32 * j + 32, 0, g, qt * P:(qt + 1) * P],
                                     stacks[own(job, b)][32 * j:32 * j + 32, 1, g, :], start=job != "A", stop=True,
                                     skip_group_check=True)
                last.then_inc(scores_ready, 1)

            def turn(h, t):
                out = turn_bank[t[1] % T_BANKS]
                before = later(t, -T_BANKS)
                wait(pe, copied_dve if before[1] % COPY_PERIOD in COPY_ON_DVE else copied_act,
                     copies(before, before[1] % COPY_PERIOD in COPY_ON_DVE))
                wait(pe, exps_ready, times(t, NT, NT))
                for qt in range(NT):
                    for kt in range(NT):
                        last = pe.transpose(out[:, kt * S + qt * P:kt * S + (qt + 1) * P],
                                            probs[:, t[1] % N_PROBS, qt, kt * P:(kt + 1) * P], identity[:])
                last.then_inc(turned, 1)

            def weigh_values(place, g, t):
                n = g % 2
                for on_dve in (False, True):
                    wait(pe, copied_dve if on_dve else copied_act, copies(t, on_dve))
                wait(pe, heads_copied, group(t))
                for kt in range(NT):
                    for j in range(HG):
                        last = pe.matmul(head_bank[32 * j:32 * j + HD + 1, n * S:(n + 1) * S],
                                         values[place][:, kt, g * HG + j, :], probsT[:, n, j, kt, :],
                                         start=kt == 0, stop=kt == NT - 1, skip_group_check=True)
                last.then_inc(heads_ready, 1)

            def dense(use, t_fin):
                stage, job, b, part = use
                if stage in NO_PSUM:
                    return
                if stage == "fin":
                    wait(pe, heads_copied, group(t_fin) + 1)
                elif stage == "oT":
                    if isinstance(b, int) and b == 0:
                        pe.wait_ge(late_weights, 2 * 16)
                    stage_taken(pe, "fin", job, b, 1)
                elif stage == "oproj":
                    stage_taken(pe, "oT", job, b, 0)
                elif stage == "qk" and job == "L":
                    stage_taken(pe, "lT", job, b, 0)
                elif stage == "qk":
                    if isinstance(b, int) and b == 0 and job == "C":
                        pe.wait_ge(weights_c, 16)
                    source = "xT" if job == "A" else "cT"
                    wait(pe, load[source], b * 16 + 16)
                elif stage == "v" and job == "L":
                    stage_taken(pe, "lT", job, b, 0)
                elif stage == "lT":
                    normalised(pe, "K", b)
                    normalised(pe, "Q", b)
                elif stage == "ffT":
                    normalised(pe, "C", b)
                elif stage == "ff1":
                    stage_taken(pe, "ffT", job, b, 0)
                elif stage == "ff2":
                    stage_taken(pe, "ff1", job, b, 0)
                    stage_taken(pe, "ff1", job, b, 1)
                out, filled = stage_free(pe, *use)
                if stage == "fin":
                    for qt in range(NT):
                        for n in range(2):
                            at = (2 * qt + n) * P
                            last = pe.transpose(out[:, at:at + P], headsT[:, 2 * part + n, qt * P:(qt + 1) * P],
                                                identity[:])
                elif stage == "oT":
                    for qt in range(NT):
                        last = pe.transpose(out[:, qt * P:(qt + 1) * P], attended[job][:, qt, :], identity[:])
                elif stage == "oproj":
                    for qt in range(NT):
                        last = pe.matmul(out[:, qt * D:(qt + 1) * D], attendedT[:, qt * P:(qt + 1) * P],
                                         weight(job + "o"), start=True, stop=True)
                elif stage == "qk":
                    q_in = lT[:, 0, :] if job == "L" else xT[:]
                    k_in = {"A": xT[:], "C": cT[:], "L": lT[:, 1, :]}[job]
                    pe.matmul(out[:, 0:S], weight(job + "q"), q_in, start=True, stop=True)
                    last = pe.matmul(out[:, S:2 * S], weight(job + "k"), k_in, start=True, stop=True)
                elif stage == "v":
                    source = {"A": xT[:], "C": cT[:], "L": lT[:, 1, :]}[job]
                    for kt in range(NT):
                        last = pe.matmul(out[:, kt * D:(kt + 1) * D], source[:, kt * P:(kt + 1) * P],
                                         weight(job + "v"), start=True, stop=True)
                elif stage == "lT":
                    for n, k in enumerate("QK"):
                        for qt in range(NT):
                            last = pe.transpose(out[:, n * S + qt * P:n * S + (qt + 1) * P], normed[k][:, qt, :],
                                                identity[:])
                elif stage == "ffT":
                    for qt in range(NT):
                        last = pe.transpose(out[:, qt * P:(qt + 1) * P], normed["C"][:, qt, :], identity[:])
                elif stage == "ff1":
                    last = hidden(out, "w1", part)
                elif stage == "ff2":
                    last = from_hidden(out, "w2", 0)
                last.then_inc(filled, 1)

            def hidden(out, w, part):
                for n in range(2):
                    at = W_FF[w] + (2 * part + n) * P
                    last = pe.matmul(out[:, n * S:(n + 1) * S], weights[:, at:at + P], ffT[:], start=True, stop=True)
                return last

            def from_hidden(out, w, buffer):
                for qt in range(NT):
                    for c in range(F // P):
                        at = W_FF[w] + c * D
                        last = pe.matmul(out[:, qt * D:(qt + 1) * D], hiddenT[:, buffer, c, qt * P:(qt + 1) * P],
                                         weights[:, at:at + D], start=c == 0, stop=c == F // P - 1)
                return last

            def warm(job, b, t0):
                for h in range(LEAD_S):
                    scores(job, b, h, later(t0, h))

            def step(h, kind, i, job, b, t0, prev, nxt):
                far = ahead(h, LEAD_S, job, b, t0, nxt)
                if far:
                    scores(*far)
                for use in stages(kind, i, h):
                    dense(use, last_head(use, t0, prev))
                if job:
                    turn(h, later(t0, h))
                if h == 1 and prev:
                    weigh_values(own(prev[0], prev[1]), NG - 1, later(prev[2], H - 1))
                elif h % HG == 1 and h > 1 and job:
                    g = h // HG - 1
                    weigh_values(own(job, b), g, later(t0, g * HG + HG - 1))

            def feed_forward(b, part):
                if part == 0:
                    pe.wait_ge(ln_steps["N"], (b + 1) * LN_STEPS["N"])
                    wait(pe, rows_copied, b)
                    for qt in range(NT):
                        last = pe.transpose(score_bank[0][:, qt * P:(qt + 1) * P], normed["A"][:, qt, :], identity[:])
                    last.then_inc(rows_turned, 1)
                elif part == 1:
                    pe.wait_ge(rows_copied, b + 1)
                    for n in range(2):
                        wait(pe, gelus_ready, b * 2 + (n - 1))
                        hidden(turn_bank[n], "fc1", n).then_inc(hidden_ready, 1)
                else:
                    pe.wait_ge(gelus_ready, b * 2 + 2)
                    wait(pe, results_ready, b)
                    from_hidden(score_bank[1], "fc2", b % 2).then_inc(out_ready, 1)

            def tick(k):
                for part in (1, 0, 2):
                    if 0 <= k - part < B:
                        feed_forward(k - part, part)

            pe.wait_ge(constants, 4 * 16)
            pe.wait_ge(const_steps, 4)
            pe.wait_ge(pads_ready, 3)
            for stage in PREPARE:
                dense((stage, "A", 0, 0), None)
            run_jobs(pe, warm, step, tick)

        @block.vector
        def _(dve):
            def maximum(job, b, h, t):
                source = score_bank[t[1] % S_BANKS]
                least = neg_max_a if job == "A" else neg_max_cl
                if job in "AC" and isinstance(b, int) and b == 0 and h % HG == 0:
                    dve.wait_ge(bias_in[job][h // HG], 16)
                if job == "L" and h == 0:
                    wait(dve, mask_ready["L"], b + 1)
                wait(dve, scores_ready, times(t, 1, 1))
                settle(dve, b)
                for qt in range(NT):
                    dve.tensor_tensor_reduce(
                        out=source[:, qt * S:(qt + 1) * S], in0=source[:, qt * S:(qt + 1) * S],
                        in1=masks[own(job, b)][:, qt, :] if job == "L" else bias[job][:, h, qt, :],
                        scale=-1.0, scalar=3.0e38,
                        op0=ALU.add, op1=ALU.min, accum_out=least[:, qt, h:h + 1]).then_inc(maxima_ready, 1)

            def copy_turned(h, t):
                n = (h // HG) % 2
                wait(dve, turned, times(t, 1, 1))
                wait(dve, heads_ready, group(t) - 1)
                dve.tensor_copy(probsT[:, n, h % HG, :, :].rearrange("p a b -> p (a b)"), turn_bank[t[1] % T_BANKS][:])\
                    .then_inc(copied_dve, 1)

            def layer_norm(k, b, source, first=0):
                done, n = ln_steps[k], b * LN_STEPS[k] + first
                for qt in range(NT):
                    dve.bn_stats(out=stats[k][:, qt, :], in_=source(qt)).then_inc(done, 1)
                for qt in range(NT):
                    dve.wait_ge(done, n + 1 + qt)
                    settle(dve, b)
                    dve.bn_aggr(out=mean_var[k][:, qt, :], in_=stats[k][:, qt, :]).then_inc(done, 1)
                dve.wait_ge(done, n + 2 * NT)
                dve.tensor_scalar(mean_var[k][:, :, 1], mean_var[k][:, :, 1], EPS, None, ALU.add).then_inc(done, 1)
                to = normed["A"] if k == "N" else normed[k]
                for qt in range(NT):
                    dve.scalar_tensor_tensor(out=to[:, qt, :], in0=source(qt), scalar=mean_var[k][:, qt, 0:1],
                                             in1=vec(f"ln_{k}_g"), op0=ALU.subtract, op1=ALU.mult).then_inc(done, 1)

            def dense(use, t_fin):
                stage, job, b, part = use
                if stage == "fin":
                    source, read = stage_full(dve, *use)
                    rows = source[:].rearrange("p (t j c) -> p t j c", t=NT, j=H // 2)
                    steps = fins_before(t_fin) * 2
                    if job == "A":
                        dve.scalar_tensor_tensor(out=sums[:], in0=neg_max_a[:, :, part * H // 2:(part + 1) * H // 2],
                                                 scalar=-MASKED / 2, in1=rows[:, :, :, HD], op0=ALU.is_lt,
                                                 op1=ALU.mult).then_inc(fin_steps, 1)
                    else:
                        dve.tensor_copy(sums[:], rows[:, :, :, HD]).then_inc(fin_steps, 1)
                    dve.wait_ge(fin_steps, steps + 1)
                    dve.reciprocal(inverse[:], sums[:]).then_inc(fin_steps, 1)
                    dve.wait_ge(fin_steps, steps + 2)
                    to = attended[job][:, :, part * D // 2:(part + 1) * D // 2]\
                        .rearrange("p t (j c) -> p t j c", j=H // 2)
                    dve.tensor_tensor(to, rows[:, :, :, 0:HD], inverse[:].unsqueeze(3).broadcast_to([P, NT, H // 2, HD]),
                                      op=ALU.mult).then_inc(read, 1)
                elif stage == "oproj":
                    source, read = stage_full(dve, *use)
                    rows = source[:, 0:NT * D].rearrange("p (t d) -> p t d", t=NT)
                    if job == "L":
                        wait(dve, res_ready["L"], b + 1)
                        dve.tensor_tensor(x2[:, b, :, :], rows, residual["L"][:], op=ALU.add).then_inc(read, 1)
                    else:
                        if job == "A":
                            wait(dve, res_ready["A"], b + 1)
                            if isinstance(b, int) and b == 0:
                                dve.wait_ge(late_weights, 2 * 16)
                        else:
                            normalised(dve, "A", b, 1)
                        dve.tensor_tensor(summed[:], rows, residual[job][:], op=ALU.add).then_inc(read, 1)
                        stage_taken(dve, *use)
                        layer_norm(job, b, lambda qt: summed[:, qt, :])
                elif stage == "split":
                    stage_taken(dve, "qk", job, b, 0)
                    for g in range(NG):
                        wait(dve, stacks_in[job][g], b * STACK_DMAS)
                    dve.tensor_copy(qk_parts[job][:, 0:4:3, :], qk_plain[:]).then_inc(split_done[job], 1)
                    dve.wait_ge(split_done[job], b * 2 + 1)
                    dve.tensor_tensor(qk_parts[job][:, 1:3, :], qk_plain[:], qk_parts[job][:, 0:4:3, :].bitcast(f32),
                                      op=ALU.subtract)\
                        .then_inc(split_done[job], 1)
                elif stage == "v" and job != "L":
                    source, read = stage_full(dve, *use)
                    dve.tensor_tensor(values[own(job, b)][:, :, :, 0:HD],
                                      source[:, 0:NT * D].rearrange("p (t h c) -> p t h c", t=NT, h=H),
                                      vec2(job + "v_b").rearrange("p t (h c) -> p t h c", h=H), op=ALU.add)\
                        .then_inc(read, 1)
                elif stage == "ff2":
                    source, read = stage_full(dve, *use)
                    rows = source[:, 0:NT * D].rearrange("p (t d) -> p t d", t=NT)
                    dve.tensor_tensor(ff_out[:], rows, vec2("ff_b2"), op=ALU.add).then_inc(read, 1)
                    stage_taken(dve, *use)
                    normalised(dve, "C", b)
                    dve.scalar_tensor_tensor(out=summed[:], in0=ff_out[:], scalar=0.0, in1=normed["C"][:],
                                             op0=ALU.max, op1=ALU.add).then_inc(ln_steps["F"], 1)
                    dve.wait_ge(ln_steps["F"], b * LN_STEPS["F"] + 1)
                    wait(dve, res_ready["L"], b * 1)
                    layer_norm("F", b, lambda qt: summed[:, qt, :], 1)
                elif stage == "lnQ":
                    normalised(dve, "F", b)
                    layer_norm("Q", b, lambda qt: normed["F"][:, qt, :])
                elif stage == "lnK":
                    dve.wait_ge(load["c"], b * 16 + 16)
                    layer_norm("K", b, lambda qt: c_tok[:, qt, :])

            def warm(job, b, t0):
                for h in range(LEAD_M):
                    maximum(job, b, h, later(t0, h))

            def step(h, kind, i, job, b, t0, prev, nxt):
                far = ahead(h, LEAD_M, job, b, t0, nxt)
                if far:
                    maximum(*far)
                for use in stages(kind, i, h):
                    dense(use, last_head(use, t0, prev))
                if job and h % COPY_PERIOD in COPY_ON_DVE:
                    copy_turned(h, later(t0, h))

            def norm_rows(b):
                stage_taken(dve, "oproj", "L", b, 0)
                wait(dve, rows_turned, b)
                layer_norm("N", b, lambda qt: x2[:, b, qt, :])
                dve.wait_ge(ln_done["N"], b * LN_PARTS["N"] + 1)
                for qt in range(NT):
                    dve.wait_ge(ln_steps["N"], b * LN_STEPS["N"] + (2 * NT + 2 + qt))
                    dve.scalar_tensor_tensor(out=normed["A"][:, qt, :], in0=normed["A"][:, qt, :],
                                             scalar=rstd["N"][:, qt:qt + 1], in1=vec("ln_N_b"), op0=ALU.mult,
                                             op1=ALU.add).then_inc(ln_steps["N"], 1)

            def add_result(b):
                dve.wait_ge(ln_done["N"], b * LN_PARTS["N"] + 2)
                dve.wait_ge(out_ready, b + 1)
                dve.tensor_tensor(x2[:, b, :, :], score_bank[1][:, 0:NT * D].rearrange("p (t d) -> p t d", t=NT),
                                  x2[:, b, :, :], op=ALU.add).then_inc(results_ready, 1)

            def tick(k):
                if k == 0:
                    norm_rows(0)
                if k + 1 < B:
                    norm_rows(k + 1)
                if 0 <= k - 2 < B:
                    add_result(k - 2)

            dve.wait_ge(constants, 4 * 16)
            dve.tensor_copy(identity16[:], identity[:]).then_inc(const_steps, 1)
            dve.memset(head_bank[:], 0.0).then_inc(const_steps, 1)
            for job in "AC":
                at = COLUMN[job + "q"]
                dve.tensor_scalar(columns[:, at:at + 1], columns[:, at:at + 1], SCALE[job], None, ALU.mult)\
                    .then_inc(const_steps, 1)
            for stage in PREPARE:
                dense((stage, "A", 0, 0), None)
            run_jobs(dve, warm, step, tick)

        @block.scalar
        def _(act):
            def exponentials(h, t, job):
                source = score_bank[t[1] % S_BANKS]
                least = neg_max_a if job == "A" else neg_max_cl
                wait(act, maxima_ready, times(t, NT, NT))
                wait(act, turned, times(t, 1, 1 - N_PROBS))
                for qt in range(NT):
                    act.activation(probs[:, t[1] % N_PROBS, qt, :], source[:, qt * S:(qt + 1) * S], ACT.Exp,
                                   bias=least[:, qt, h:h + 1], scale=-1.0).then_inc(exps_ready, 1)

            def copy_turned(h, t):
                n = (h // HG) % 2
                wait(act, turned, times(t, 1, 1))
                wait(act, heads_ready, group(t) - 1)
                act.activation(probsT[:, n, h % HG, :, :].rearrange("p a b -> p (a b)"), turn_bank[t[1] % T_BANKS][:],
                               ACT.Copy).then_inc(copied_act, 1)

            def copy_heads(t, g):
                n = g % 2
                wait(act, heads_ready, group(t) + 1)
                act.activation(headsT[:, g, :], head_bank[:, n * S:(n + 1) * S], ACT.Copy).then_inc(heads_copied, 1)

            def dense(use):
                stage, job, b, part = use
                if stage == "qk":
                    source, read = stage_full(act, *use)
                    if job == "L":
                        act.activation(qk_plain[:, 0, :], source[:, 0:S], ACT.Copy, scale=SCALE[job])
                        act.activation(qk_plain[:, 1, :], source[:, S:2 * S], ACT.Copy).then_inc(read, 1)
                    else:
                        at = COLUMN[job + "q"]
                        act.activation(qk_plain[:, 0, :], source[:, 0:S], ACT.Identity, bias=columns[:, at:at + 1],
                                       scale=SCALE[job])
                        act.activation(qk_plain[:, 1, :], source[:, S:2 * S], ACT.Identity,
                                       bias=columns[:, at + 1:at + 2]).then_inc(read, 1)
                elif stage == "v" and job == "L":
                    source, read = stage_full(act, *use)
                    act.activation(values[own(job, b)][:, :, :, 0:HD],
                                   source[:, 0:NT * D].rearrange("p (t h c) -> p t h c", t=NT, h=H), ACT.Copy)\
                        .then_inc(read, 1)
                elif stage in ("oT", "ffT"):
                    source, read = stage_full(act, *use)
                    act.activation((attendedT if stage == "oT" else ffT)[:], source[:, 0:S], ACT.Copy).then_inc(read, 1)
                elif stage == "lT":
                    source, read = stage_full(act, *use)
                    act.activation(lT[:].rearrange("p a s -> p (a s)"), source[:], ACT.Copy).then_inc(read, 1)
                elif stage == "ff1":
                    source, read = stage_full(act, *use)
                    hidden(source, part, ACT.Relu, "b1", 0).then_inc(read, 1)

            def hidden(source, part, func, bias_name, buffer):
                for n in range(2):
                    c = 2 * part + n
                    at = COLUMN[bias_name] + c
                    last = act.activation(hiddenT[:, buffer, c, :], source[:, n * S:(n + 1) * S], func,
                                          bias=columns[:, at:at + 1])
                return last

            def warm(job, b, t0):
                for h in range(LEAD_E):
                    exponentials(h, later(t0, h), job)

            def step(h, kind, i, job, b, t0, prev, nxt):
                far = ahead(h, LEAD_E, job, b, t0, nxt)
                if far:
                    exponentials(far[2], far[3], far[0])
                for use in stages(kind, i, h):
                    dense(use)
                if job and h % COPY_PERIOD not in COPY_ON_DVE:
                    copy_turned(h, later(t0, h))
                if h == 2 and prev:
                    copy_heads(later(prev[2], H - 1), NG - 1)
                elif h % HG == 2 and h > 2 and job:
                    copy_heads(later(t0, (h // HG - 1) * HG), h // HG - 1)

            def copy_rows(b):
                act.wait_ge(rows_turned, b + 1)
                wait(act, hidden_ready, b * 2)
                act.activation(ffT[:], score_bank[0][:, 0:S], ACT.Copy).then_inc(rows_copied, 1)

            def gelus(b):
                wait(act, out_ready, b - 1)
                for n in range(2):
                    act.wait_ge(hidden_ready, b * 2 + (n + 1))
                    hidden(turn_bank[n], n, ACT.Gelu, "fc1_b", b % 2).then_inc(gelus_ready, 1)

            def tick(k):
                if 0 <= k - 1 < B:
                    gelus(k - 1)
                if k < B:
                    copy_rows(k)

            act.wait_ge(halves_ready, 1)
            act.activation(warm_up[:], minus_half[:], ACT.Exp)
            act.wait_ge(constants, 4 * 16)
            act.wait_ge(const_steps, 4)
            for stage in PREPARE:
                dense((stage, "A", 0, 0))
            run_jobs(act, warm, step, tick)

        @block.gpsimd
        def _(pool):
            def normalise(k, b):
                to, n = normed[k], b * LN_PARTS[k]
                wait(pool, ln_steps[k], b * LN_STEPS[k] + (LN_STEPS[k] - NT))
                pool.tensor_tensor(rstd[k][:], mean_var[k][:, :, 1], minus_half[:], op=ALU.pow).then_inc(ln_done[k], 1)
                wait(pool, ln_done[k], n + 1)
                wait(pool, ln_steps[k], b * LN_STEPS[k] + LN_STEPS[k])
                pool.tensor_tensor(to[:], to[:], rstd[k][:].unsqueeze(2).broadcast_to([P, NT, D]), op=ALU.mult)\
                    .then_inc(ln_done[k], 1)
                wait(pool, ln_done[k], n + 2)
                pool.tensor_tensor(to[:], to[:], vec2(f"ln_{k}_b"), op=ALU.add).then_inc(ln_done[k], 1)

            def dense(use, t_before):
                stage, job, b, part = use
                if stage == "maskA":
                    wait(pool, load["mask_a"], b * 16 + 16)
                    if t_before:
                        wait(pool, scores_ready, times(t_before))
                    settle(pool, b)
                    pool.tensor_scalar(mask_a[:], mask_a8[:], MASKED, None, ALU.mult).then_inc(mask_ready["A"], 1)
                elif stage == "maskL":
                    wait(pool, load["mask_l"], b * 16 + 16)
                    if t_before:
                        wait(pool, maxima_ready, times(t_before, NT))
                    settle(pool, b)
                    pool.tensor_scalar(masks[own("L", b)][:], mask_l8[:], MASKED, None, ALU.mult)\
                        .then_inc(mask_ready["L"], 1)
                elif stage == "resA":
                    wait(pool, load["x"], b * 16 + 16)
                    wait(pool, ln_steps["A"], b * LN_STEPS["A"] - 3 * NT)
                    pool.tensor_tensor(residual["A"][:], x_tok[:], vec2("Ao_b"), op=ALU.add)\
                        .then_inc(res_ready["A"], 1)
                elif stage == "oproj" and job in "AC":
                    normalise(job, b)
                    if job == "A":
                        normalised(pool, "A", b)
                        pool.tensor_tensor(residual["C"][:], normed["A"][:], vec2("Co_b"), op=ALU.add)\
                            .then_inc(ln_done["A"], 1)
                elif stage == "ff2":
                    normalise("F", b)
                elif stage in ("lnQ", "lnK"):
                    normalise(job, b)
                elif stage == "resL":
                    if not isinstance(b, int) or b > 0:
                        stage_taken(pool, "oproj", "L", b - 1, 0)
                    normalised(pool, "F", b)
                    pool.tensor_tensor(residual["L"][:], normed["F"][:], vec2("Lo_b"), op=ALU.add)\
                        .then_inc(res_ready["L"], 1)

            def step(h, kind, i, job, b, t0, prev, nxt):
                for use in stages(kind, i, h):
                    dense(use, later(prev[2], H) if prev else None)

            def rows(b):
                pool.wait_ge(ln_steps["N"], b * LN_STEPS["N"] + (2 * NT + 1))
                pool.tensor_tensor(rstd["N"][:], mean_var["N"][:, :, 1], minus_half[:], op=ALU.pow)\
                    .then_inc(ln_done["N"], 1)
                pool.wait_ge(ln_steps["N"], b * LN_STEPS["N"] + (3 * NT + 1))
                pool.tensor_tensor(x2[:, b, :, :], x2[:, b, :, :], vec2("fc2_b"), op=ALU.add).then_inc(ln_done["N"], 1)

            def tick(k):
                if k == 0:
                    rows(0)
                if k + 1 < B:
                    rows(k + 1)

            pool.memset(minus_half[:], -0.5).then_inc(halves_ready, 1)
            pool.wait_ge(halves_ready, 1)
            for job in "ACL":
                pool.memset(values[job][:, :, :, HD:HD + 1], 1.0).then_inc(pads_ready, 1)
            dense(("maskA", "A", 0, 0), None)
            pool.wait_ge(late_weights, 2 * 16)
            dense(("resA", "A", 0, 0), None)
            run_jobs(pool, lambda *_: None, step, tick)


def kernel(**inputs):
    import numpy as np
    import concourse.bacc as bacc
    from concourse.bass_utils import run_bass_kernel_spmd

    a = {k: np.asarray(v) for k, v in inputs.items()}
    l0, l1 = "L0_xattn_", "L1_xattn_"
    kv = a[l1 + "kv_w"]
    square = [a[l0 + "sa_wq"], a[l0 + "sa_wk"], a[l0 + "sa_wv"], a[l0 + "ca_wq"], a[l0 + "ca_wk"], a[l0 + "ca_wv"],
              a[l0 + "sa_wo"], a[l0 + "ca_wo"], a[l1 + "q_w"], kv[:, :D], kv[:, D:], a[l1 + "proj_w"]]

    def by_rows(w):
        return w.reshape(F // P, P, D).transpose(1, 0, 2).reshape(P, F)

    weights = np.concatenate(square + [a[l0 + "ff_w1"], by_rows(a[l0 + "ff_w2"]), a[l1 + "fc1_w"],
                                       by_rows(a[l1 + "fc2_w"])], axis=1)
    columns = np.concatenate([a[l0 + n].reshape(-1, P) for n in ("sa_bq", "sa_bk", "ca_bq", "ca_bk", "ff_b1")]
                             + [a[l1 + "fc1_b"].reshape(-1, P)], axis=0).T
    names = {"Av_b": l0 + "sa_bv", "Cv_b": l0 + "ca_bv", "Ao_b": l0 + "sa_bo", "Co_b": l0 + "ca_bo",
             "Lo_b": l1 + "proj_b", "ln_A_g": l0 + "sa_g", "ln_A_b": l0 + "sa_b", "ln_C_g": l0 + "ca_g",
             "ln_C_b": l0 + "ca_b", "ln_F_g": l0 + "ff_g", "ln_F_b": l0 + "ff_b", "ln_Q_g": l1 + "qn_w",
             "ln_Q_b": l1 + "qn_b", "ln_K_g": l1 + "cn_w", "ln_K_b": l1 + "cn_b", "ln_N_g": l1 + "n2_w",
             "ln_N_b": l1 + "n2_b", "ff_b2": l0 + "ff_b2", "fc2_b": l1 + "fc2_b"}
    arrays = {
        "x": a["x"], "x_turned": a["x"].transpose(0, 2, 1),
        "ctx": a["ctx_1024"], "ctx_turned": a["ctx_1024"].transpose(0, 2, 1),
        "mask_self": a["mask_BxSxS2_bk1"], "mask_cross": a["mask_BxSxS2_bk0"],
        "bias_self": a["fside_1x16xSxS2_0"][0], "bias_cross": a[l0 + "attn_2d_bias"][0],
        "weights": weights, "columns": columns, "vectors": np.stack([a[names[n]] for n in VECTORS]),
        "identity": np.eye(P, dtype=np.float32),
    }
    nc = bacc.Bacc("TRN2", target_bir_lowering=False, num_devices=1)
    args = []
    for name in arrays:
        arrays[name] = np.ascontiguousarray(arrays[name])
        args.append(nc.dram_tensor("in_" + name, arrays[name].shape, mybir.dt.from_np(arrays[name].dtype),
                                   kind="ExternalInput").ap())
    args.append(nc.dram_tensor("out", (B, S, D), mybir.dt.float32, kind="ExternalOutput").ap())
    two_layers(nc, *args)
    r = run_bass_kernel_spmd(nc, [{"in_" + n: v for n, v in arrays.items()}], core_ids=[0])
    return r.results[0]["out"]
```
